# Optimizing a Trainium2 kernel written in Bass

```python
import numpy as np
import jax
import jax.numpy as jnp

def _softmax(x, axis=-1):
    return jax.nn.softmax(x, axis=axis)

def _gelu(x):
    return jax.nn.gelu(x, approximate=True)

def _silu(x):
    return jax.nn.silu(x)

def _sigmoid(x):
    return jax.nn.sigmoid(x)

def _layernorm(x, axis=-1, eps=1e-05):
    m = jnp.mean(x, axis=axis, keepdims=True)
    v = jnp.var(x, axis=axis, keepdims=True)
    return (x - m) / jnp.sqrt(v + eps)

def _scatter_add(tgt, idx, src, axis=0):
    return tgt.at[idx].add(src)

def _segment_sum(src, seg, n):
    return jax.ops.segment_sum(src, seg, n)
kernel_name = 'mk_recurrent_d2_jaxref_r8_0ba7a1'

def setup_inputs(seed: int=0):
    np.random.seed(seed)
    _w = jnp.asarray

    def _L0_attn_setup():
        import jax, jax.numpy as jnp
        import numpy as np
        NEG_INF = -1e+30

        def rotary_pos_emb(x):
            B, T, H, D = x.shape
            exponents = (jnp.arange(0, D, 2)[:D // 2] // D).astype(jnp.float32)
            freqs = 1.0 / jnp.power(jnp.float32(1000.0), exponents)
            theta = jnp.arange(T, dtype=jnp.float32)[:, None] * freqs[None, :]
            cos = jnp.cos(theta)[None, :, None, :]
            sin = jnp.sin(theta)[None, :, None, :]
            xr = x.astype(jnp.float32).reshape(B, T, H, D // 2, 2)
            x0, x1 = (xr[..., 0], xr[..., 1])
            out = jnp.stack([x0 * cos - x1 * sin, x0 * sin + x1 * cos], axis=-1)
            return out.reshape(B, T, H, D).astype(x.dtype)

        def attention_fwd(x, wq, wk, wv, wo, n_heads=32):
            B, T, C = x.shape
            hd = C // n_heads
            xq = (x @ wq.T).reshape(B, T, n_heads, hd)
            xk = (x @ wk.T).reshape(B, T, n_heads, hd)
            xv = (x @ wv.T).reshape(B, T, n_heads, hd)
            xq = rotary_pos_emb(xq)
            xk = rotary_pos_emb(xk)
            scale = hd ** (-0.5)
            scores = jnp.einsum('bqhd,bkhd->bhqk', xq, xk) * scale
            causal = jnp.tril(jnp.ones((T, T), dtype=bool))
            scores = jnp.where(causal[None, None], scores, NEG_INF)
            probs = jax.nn.softmax(scores.astype(jnp.float32), axis=-1).astype(xq.dtype)
            out = jnp.einsum('bhqk,bkhd->bqhd', probs, xv).reshape(B, T, C)
            return out @ wo.T
        key = jax.random.key(seed)
        ks = jax.random.split(key, 5)
        B, T, C = (2, 256, 512)
        s = 0.02
        return {'x': jax.random.normal(ks[0], (B, T, C), jnp.float32), 'wq': jax.random.normal(ks[1], (C, C), jnp.float32) * s, 'wk': jax.random.normal(ks[2], (C, C), jnp.float32) * s, 'wv': jax.random.normal(ks[3], (C, C), jnp.float32) * s, 'wo': jax.random.normal(ks[4], (C, C), jnp.float32) * s}
    _L0_attn_in = _L0_attn_setup()

    def _L0_ffn_setup():
        import jax, jax.numpy as jnp
        import numpy as np
        NUM_EXPERTS = 8
        D_IN = 512
        D_OUT = 512
        key = jax.random.key(seed)
        k_x, k_gw, k_gb, k_ew, k_eb = jax.random.split(key, 5)
        x = jax.random.normal(k_x, (4, 256, D_IN), dtype=jnp.float32)
        gate_w = jax.random.normal(k_gw, (NUM_EXPERTS, D_IN), dtype=jnp.float32) * 0.02
        gate_b = jax.random.normal(k_gb, (NUM_EXPERTS,), dtype=jnp.float32) * 0.02
        expert_w = jax.random.normal(k_ew, (NUM_EXPERTS, D_OUT, D_IN), dtype=jnp.float32) * 0.02
        expert_b = jax.random.normal(k_eb, (NUM_EXPERTS, D_OUT), dtype=jnp.float32) * 0.02
        return {'x': x, 'gate_w': gate_w, 'gate_b': gate_b, 'expert_w': expert_w, 'expert_b': expert_b}
    _L0_ffn_in = _L0_ffn_setup()

    def _L1_attn_setup():
        import jax, jax.numpy as jnp
        import numpy as np
        HIDDEN = 512
        N_HEADS = 32
        N_KV = 8
        HEAD_DIM = HIDDEN // N_HEADS
        Q_PER_KV = N_HEADS // N_KV
        SEQ = 256
        ROPE_BASE = 1000000.0
        POS_SCALE = 1.0
        SM_SCALE = 1.0 / HEAD_DIM
        BLOCK = 64
        LOCAL_BLOCKS = 16
        VERT_STRIDE = 8

        def _blocksparse_mask(seq_len):
            nb = seq_len // BLOCK
            qb = np.arange(nb)[:, None]
            kb = np.arange(nb)[None, :]
            bmask = (kb <= qb) & ((qb - kb < LOCAL_BLOCKS) | ((kb + 1) % VERT_STRIDE == 0))
            emask = np.kron(bmask, np.ones((BLOCK, BLOCK), dtype=bool))
            i = np.arange(seq_len)
            emask &= i[:, None] >= i[None, :]
            return jnp.asarray(emask)

        def _rope(x, cos, sin):
            x1, x2 = jnp.split(x, 2, axis=-1)
            rot = jnp.concatenate([-x2, x1], axis=-1)
            return x * cos[None, :, None, :] + rot * sin[None, :, None, :]
        key = jax.random.key(seed)
        k1, k2, k3, k4, k5 = jax.random.split(key, 5)
        qkv_out = (N_HEADS + 2 * N_KV) * HEAD_DIM
        return {'hidden_states': jax.random.normal(k1, (1, SEQ, HIDDEN), dtype=jnp.float32), 'w_qkv': jax.random.normal(k2, (qkv_out, HIDDEN), dtype=jnp.float32) * 0.02, 'b_qkv': jnp.zeros((qkv_out,), dtype=jnp.float32), 'w_dense': jax.random.normal(k3, (HIDDEN, HIDDEN), dtype=jnp.float32) * 0.02, 'b_dense': jnp.zeros((HIDDEN,), dtype=jnp.float32)}
    _L1_attn_in = _L1_attn_setup()

    def _L1_ffn_setup():
        import jax, jax.numpy as jnp
        import numpy as np
        LORA_SCALE = 16.0 / jnp.sqrt(16.0)
        TOP_K = 2
        key = jax.random.key(seed)
        k1, k2, k3, k4 = jax.random.split(key, 4)
        B_, S, D, O, E, R = (4, 256, 512, 512, 4, 16)
        x = jax.random.normal(k1, (B_, S, D), dtype=jnp.float32)
        router_w = jax.random.normal(k2, (E, D), dtype=jnp.float32) * 0.02
        A = jax.random.normal(k3, (E, R, D), dtype=jnp.float32) * 0.02
        B = jax.random.normal(k4, (O,), dtype=jnp.float32)
        B = jax.random.normal(k4, (E, O, R), dtype=jnp.float32) * 0.02
        return {'x': x, 'router_w': router_w, 'A': A, 'B': B}
    _L1_ffn_in = _L1_ffn_setup()
    _d = {'L0_attn_x': _L0_attn_in['x'], 'L0_attn_wq': _L0_attn_in['wq'], 'L0_attn_wk': _L0_attn_in['wk'], 'L0_attn_wv': _L0_attn_in['wv'], 'L0_attn_wo': _L0_attn_in['wo'], 'L0_ffn_gate_w': _L0_ffn_in['gate_w'], 'L0_ffn_gate_b': _L0_ffn_in['gate_b'], 'L0_ffn_expert_w': _L0_ffn_in['expert_w'], 'L0_ffn_expert_b': _L0_ffn_in['expert_b'], 'L1_attn_w_qkv': _L1_attn_in['w_qkv'], 'L1_attn_b_qkv': _L1_attn_in['b_qkv'], 'L1_attn_w_dense': _L1_attn_in['w_dense'], 'L1_attn_b_dense': _L1_attn_in['b_dense'], 'L1_ffn_router_w': _L1_ffn_in['router_w'], 'L1_ffn_A': _L1_ffn_in['A'], 'L1_ffn_B': _L1_ffn_in['B']}
    _x0 = _d['L0_attn_x']
    _d['L0_attn_x'] = jax.random.normal(jax.random.fold_in(jax.random.key(seed), 1), (4, 256, 512), dtype=_x0.dtype)
    del _x0
    return _d

def reference(L0_attn_x, L0_attn_wq, L0_attn_wk, L0_attn_wv, L0_attn_wo, L0_ffn_gate_w, L0_ffn_gate_b, L0_ffn_expert_w, L0_ffn_expert_b, L1_attn_w_qkv, L1_attn_b_qkv, L1_attn_w_dense, L1_attn_b_dense, L1_ffn_router_w, L1_ffn_A, L1_ffn_B):

    def _L0_attn_ref(x, wq, wk, wv, wo):
        import jax, jax.numpy as jnp
        import numpy as np
        NEG_INF = -1e+30

        def rotary_pos_emb(x):
            B, T, H, D = x.shape
            exponents = (jnp.arange(0, D, 2)[:D // 2] // D).astype(jnp.float32)
            freqs = 1.0 / jnp.power(jnp.float32(1000.0), exponents)
            theta = jnp.arange(T, dtype=jnp.float32)[:, None] * freqs[None, :]
            cos = jnp.cos(theta)[None, :, None, :]
            sin = jnp.sin(theta)[None, :, None, :]
            xr = x.astype(jnp.float32).reshape(B, T, H, D // 2, 2)
            x0, x1 = (xr[..., 0], xr[..., 1])
            out = jnp.stack([x0 * cos - x1 * sin, x0 * sin + x1 * cos], axis=-1)
            return out.reshape(B, T, H, D).astype(x.dtype)

        def attention_fwd(x, wq, wk, wv, wo, n_heads=32):
            B, T, C = x.shape
            hd = C // n_heads
            xq = (x @ wq.T).reshape(B, T, n_heads, hd)
            xk = (x @ wk.T).reshape(B, T, n_heads, hd)
            xv = (x @ wv.T).reshape(B, T, n_heads, hd)
            xq = rotary_pos_emb(xq)
            xk = rotary_pos_emb(xk)
            scale = hd ** (-0.5)
            scores = jnp.einsum('bqhd,bkhd->bhqk', xq, xk) * scale
            causal = jnp.tril(jnp.ones((T, T), dtype=bool))
            scores = jnp.where(causal[None, None], scores, NEG_INF)
            probs = jax.nn.softmax(scores.astype(jnp.float32), axis=-1).astype(xq.dtype)
            out = jnp.einsum('bhqk,bkhd->bqhd', probs, xv).reshape(B, T, C)
            return out @ wo.T
        return attention_fwd(x, wq, wk, wv, wo)

    def _L0_ffn_ref(x, gate_w, gate_b, expert_w, expert_b):
        import jax, jax.numpy as jnp
        import numpy as np
        NUM_EXPERTS = 8
        D_IN = 512
        D_OUT = 512
        orig_shape = x.shape
        xf = x.reshape(-1, x.shape[-1])
        gate_logits = xf @ gate_w.T + gate_b
        gates = jax.nn.softmax(gate_logits, axis=-1)
        selected = jnp.argmax(gates, axis=-1)
        out = jnp.zeros((xf.shape[0], expert_w.shape[1]), dtype=xf.dtype)
        for j in range(expert_w.shape[0]):
            yj = xf @ expert_w[j].T + expert_b[j]
            out = out + jnp.where((selected == j)[:, None], yj, 0.0)
        return out.reshape(*orig_shape[:-1], expert_w.shape[1])

    def _L1_attn_ref(hidden_states, w_qkv, b_qkv, w_dense, b_dense):
        import jax, jax.numpy as jnp
        import numpy as np
        HIDDEN = 512
        N_HEADS = 32
        N_KV = 8
        HEAD_DIM = HIDDEN // N_HEADS
        Q_PER_KV = N_HEADS // N_KV
        SEQ = 256
        ROPE_BASE = 1000000.0
        POS_SCALE = 1.0
        SM_SCALE = 1.0 / HEAD_DIM
        BLOCK = 64
        LOCAL_BLOCKS = 16
        VERT_STRIDE = 8

        def _blocksparse_mask(seq_len):
            nb = seq_len // BLOCK
            qb = np.arange(nb)[:, None]
            kb = np.arange(nb)[None, :]
            bmask = (kb <= qb) & ((qb - kb < LOCAL_BLOCKS) | ((kb + 1) % VERT_STRIDE == 0))
            emask = np.kron(bmask, np.ones((BLOCK, BLOCK), dtype=bool))
            i = np.arange(seq_len)
            emask &= i[:, None] >= i[None, :]
            return jnp.asarray(emask)

        def _rope(x, cos, sin):
            x1, x2 = jnp.split(x, 2, axis=-1)
            rot = jnp.concatenate([-x2, x1], axis=-1)
            return x * cos[None, :, None, :] + rot * sin[None, :, None, :]
        B, S, _ = hidden_states.shape
        qkv = jnp.einsum('bsh,oh->bso', hidden_states, w_qkv) + b_qkv
        qkv = qkv.reshape(B, S, N_KV, Q_PER_KV + 2, HEAD_DIM)
        q = qkv[:, :, :, :Q_PER_KV].reshape(B, S, N_HEADS, HEAD_DIM)
        k = qkv[:, :, :, Q_PER_KV]
        v = qkv[:, :, :, Q_PER_KV + 1]
        inv_freq = 1.0 / ROPE_BASE ** (jnp.arange(0, HEAD_DIM, 2, dtype=jnp.float32) / HEAD_DIM)
        t = jnp.arange(S, dtype=jnp.float32) * POS_SCALE
        freqs = jnp.outer(t, inv_freq)
        emb = jnp.concatenate([freqs, freqs], axis=-1)
        cos, sin = (jnp.cos(emb), jnp.sin(emb))
        q = _rope(q, cos, sin)
        k = _rope(k, cos, sin)
        k = jnp.repeat(k, Q_PER_KV, axis=2)
        v = jnp.repeat(v, Q_PER_KV, axis=2)
        mask = _blocksparse_mask(S)
        scores = jnp.einsum('bqhd,bkhd->bhqk', q, k) * SM_SCALE
        scores = jnp.where(mask[None, None], scores, jnp.finfo(scores.dtype).min)
        probs = jax.nn.softmax(scores, axis=-1)
        ctx = jnp.einsum('bhqk,bkhd->bqhd', probs, v).reshape(B, S, HIDDEN)
        out = jnp.einsum('bsh,oh->bso', ctx, w_dense) + b_dense
        return out

    def _L1_ffn_ref(x, router_w, A, B):
        import jax, jax.numpy as jnp
        import numpy as np
        LORA_SCALE = 16.0 / jnp.sqrt(16.0)
        TOP_K = 2
        D = x.shape[-1]
        flat = x.reshape(-1, D)
        logits = flat @ router_w.T
        topk_vals, topk_idx = jax.lax.top_k(logits, TOP_K)
        sparse = jnp.full_like(logits, -jnp.inf)
        rows = jnp.arange(logits.shape[0])[:, None]
        sparse = sparse.at[rows, topk_idx].set(topk_vals)
        gates = jax.nn.softmax(sparse, axis=-1)
        mid = jnp.einsum('tf,erf->ter', flat, A)
        all_deltas = jnp.einsum('ter,eor->teo', mid, B) * LORA_SCALE
        delta = jnp.einsum('te,teo->to', gates, all_deltas)
        return delta.reshape(*x.shape[:-1], -1)
    x = L0_attn_x
    xn = _layernorm(x, axis=-1)
    s = _L0_attn_ref(xn, L0_attn_wq, L0_attn_wk, L0_attn_wv, L0_attn_wo)
    g = _silu(_L0_ffn_ref(xn, L0_ffn_gate_w, L0_ffn_gate_b, L0_ffn_expert_w, L0_ffn_expert_b))
    x = x + s * g
    xn = _layernorm(x, axis=-1)
    s = _L1_attn_ref(xn, L1_attn_w_qkv, L1_attn_b_qkv, L1_attn_w_dense, L1_attn_b_dense)
    g = _silu(_L1_ffn_ref(xn, L1_ffn_router_w, L1_ffn_A, L1_ffn_B))
    x = x + s * g
    return x

_drawn_inputs = setup_inputs


def setup_inputs(seed=0):
    import zlib

    import numpy as np

    out = dict(_drawn_inputs(seed))
    spreads = {'L1_attn_b_qkv': (0.0, 0.8), 'L1_attn_b_dense': (0.0, 0.8)}
    factors = {'L0_attn_wq': 8.0,
     'L0_attn_wk': 8.0,
     'L0_attn_wv': 7.081,
     'L0_attn_wo': 7.259,
     'L0_ffn_gate_w': 7.894,
     'L0_ffn_gate_b': 8.0,
     'L0_ffn_expert_w': 7.295,
     'L0_ffn_expert_b': 8.0,
     'L1_attn_w_qkv': 8.0,
     'L1_attn_w_dense': 8.0,
     'L1_ffn_router_w': 8.0,
     'L1_ffn_A': 8.0,
     'L1_ffn_B': 8.0}
    for name, (base, spread) in spreads.items():
        noise = np.random.default_rng([zlib.crc32(name.encode()), seed]).standard_normal(out[name].shape)
        drawn = base * np.exp(spread * noise) if base else spread * noise
        out[name] = jnp.asarray(drawn.astype(out[name].dtype))
    for name, factor in factors.items():
        out[name] = (out[name] * factor).astype(out[name].dtype)
    return out
```

```python
from contextlib import ExitStack

import numpy as np

import concourse.bass as bass
from concourse import mybir
from concourse.alu_op_type import AluOpType as ALU

F32 = mybir.dt.float32
F16 = mybir.dt.float16
BF16 = mybir.dt.bfloat16
U32 = mybir.dt.uint32
ACT = mybir.ActivationFunctionType
AX = mybir.AxisListType

BATCH, SEQ, C = 4, 256, 512
P = 128
TILES = SEQ // P
CH = C // P
HEADS, HD = 32, 16
KV_HEADS = 8
GROUP = 4
PAIRS = GROUP // 2
GROUPS = HEADS // GROUP
BLK = 64
MAXROW = 3 * HD
VW = 2 * HD + 1
EXPERTS = 8
RANK, LORA = 16, 4
LORA_SCALE = 16.0 / RANK ** 0.5
EPS = 1e-5
NEG = -1e30

XS, WS = 16.0, 128.0
OUT = 1.0 / (XS * WS)

W_QKV0, W_O0, W_EXP, W_QKV1, W_O1 = 1536, 512, EXPERTS * 512, 768, 512
ROUTER_AT = EXPERTS
A_AT = EXPERTS + 4
W_SMALL = A_AT + 64


def build(nc, a):
    ctx = ExitStack()
    with ctx:
        def sb(name, shape, dt=F32):
            return ctx.enter_context(nc.sbuf_tensor(name, shape, dt))

        def ps(name, shape, dt=F32):
            return ctx.enter_context(nc.psum_tensor(name, shape, dt))

        w_qkv0 = sb("w_qkv0", [P, 2, CH, W_QKV0], F16)
        w_o0 = sb("w_o0", [P, 2, CH, W_O0], F16)
        w_exp = sb("w_exp", [P, 2, CH, W_EXP], F16)
        w_qkv1 = sb("w_qkv1", [P, 2, CH, W_QKV1], F16)
        w_o1 = sb("w_o1", [P, 2, CH, W_O1], F16)
        w_small = sb("w_small", [P, 2, CH, W_SMALL], F16)
        w_b = sb("w_b", [P, 2, 512], F16)
        bias_e = sb("bias_e", [EXPERTS, 2, 512], F16)

        ident32 = sb("ident32", [P, P])
        ident16 = sb("ident16", [P, P], F16)
        identb = sb("identb", [P, P], BF16)
        mask_qk = sb("mask_qk", [P, GROUP, P], BF16)
        mask_kq = sb("mask_kq", [P, GROUP, P], BF16)
        rope0 = sb("rope0", [P, TILES, 3])
        cos1 = sb("cos1", [P, TILES, HD])
        sin1 = sb("sin1", [P, TILES, HD])
        bias_qkv1 = sb("bias_qkv1", [P, W_QKV1])
        bias_o1 = sb("bias_o1", [P, 512])
        gate_bias = sb("gate_bias", [P, EXPERTS])
        iota8 = sb("iota8", [P, 8])
        minus_half = sb("minus_half", [P, TILES])

        x = sb("x", [P, TILES, C])
        xn = sb("xn", [P, TILES, C])
        stats = sb("stats", [P, TILES, 6])
        mv = sb("mv", [P, TILES, 2])
        var_eps = sb("var_eps", [P, TILES])
        rstd = sb("rstd", [P, TILES])
        xT = sb("xT", [P, 2, CH, SEQ], F16)
        aT = sb("aT", [P, 2, CH, SEQ], F16)
        rot = sb("rot", [P, 1024])
        qk = sb("qk", [P, 1024])
        qkv1 = sb("qkv1", [P, W_QKV1])
        qs = sb("qs", [P, TILES, HEADS, BLK], F16)
        ks0 = sb("ks0", [P, TILES, HEADS, BLK], F16)
        ks1 = ks0[:, :, 0:2 * KV_HEADS, :]
        vs = sb("vs", [P, TILES, HEADS, VW], F16)
        qT = sb("qT", [P, PAIRS, SEQ], F16)
        qmT = sb("qmT", [P, PAIRS, SEQ], F16)
        kT = sb("kT", [P, PAIRS, 2, SEQ], F16)
        neg_max = sb("neg_max", [P, TILES, GROUP])
        p32 = sb("p32", [P, 3 * 512])
        p_hi = sb("p_hi", [P, 3 * 512], F16)
        p_lo = sb("p_lo", [P, 3 * 512], F16)
        recip = sb("recip", [P, TILES, GROUP])
        o_lo = sb("o_lo", [P, TILES, GROUP, HD])
        o_sum = sb("o_sum", [P, TILES, GROUP, HD])
        attn = xn
        ffn = sb("ffn", [P, TILES, C])
        th = sb("th", [P, TILES, C])
        logits = sb("logits", [P, TILES, 8])
        top = sb("top", [P, TILES, 8])
        top_at = sb("top_at", [P, TILES, 8], U32)
        top_f = sb("top_f", [P, TILES, 2])
        chosen = sb("chosen", [P, TILES, EXPERTS])
        chosen16 = sb("chosen16", [P, TILES, EXPERTS], F16)
        chosenT = sb("chosenT", [EXPERTS, SEQ], F16)
        r_bias = sb("r_bias", [P, TILES])
        r_exp = sb("r_exp", [P, TILES, LORA])
        r_sel = sb("r_sel", [P, TILES, LORA])
        r_gate = sb("r_gate", [P, TILES, LORA])
        r_sum = sb("r_sum", [P, TILES])
        r_rec = sb("r_rec", [P, TILES])
        mid = sb("mid", [P, TILES, LORA * RANK])
        mid16 = sb("mid16", [P, TILES, 2, LORA * RANK], F16)
        midT = sb("midT", [P, SEQ], F16)
        slots = [half[:, t, :, :].rearrange("p h k -> p (h k)").bitcast(F32) for half in (qs, ks0) for t in range(TILES)]

        psA = ps("psA", [P, 3, 512])
        psB = ps("psB", [P, 3, 512])
        psO = ps("psO", [P, 512])
        psW = ps("psW", [P, 512])
        tA = psA[:, 0, :].bitcast(F16)
        tW = psW[:, :].bitcast(F16)
        o_ps = psO[:, 0:TILES * GROUP * VW].rearrange("p (t h v) -> p t h v", t=TILES, h=GROUP)
        delta_ps = [psW[:, :], psO[:, :]]
        qkv_ps = [psB, psA]

        names = """const staged0 staged1 staged2 staged3 w_hi w_lo made cleared masks
            x_in x_out bn mv var rstd xn xt_ps xt_hi xt_lo proj small
            rot rope qk_hi qk_lo v_hi v_lo qkv1 cosx
            logits top top_at top_f chosen chosen_T chosenT ffn_bias ffn_in expert mixed
            t1 q_t k_t s_ps neg_max max_hi max_lo t2 qm_t st p32 p_hi p_lo pv recip o_lo o_sum attn
            at_ps at_hi at_lo out th gated weighed resid
            r_top r_top_at r_top_f r_bias r_exp r_first r_sel r_eg r_sum r_rec r_gate mid mid_hi mid_lo mid_ps midT delta ffn1 s1"""
        s = {n: ctx.enter_context(nc.semaphore("s_" + n)) for n in names.split()}
        block = ctx.enter_context(nc.Block())

        def pieces():
            for dst, src, width in ((w_qkv0, a["wqkv0"], W_QKV0), (w_qkv1, a["wqkv1"], W_QKV1), (w_o0, a["wo0"], W_O0),
                                    (w_o1, a["wo1"], W_O1), (w_exp, a["wexp"], W_EXP)):
                for c in range(CH):
                    for lo in range(0, width, 1024):
                        hi = min(lo + 1024, width)
                        yield dst[:, :, c, lo:hi], [(src[c * P:(c + 1) * P, lo:hi], 0, P, 0, hi - lo)]
            for c in range(CH):
                rows = slice(c * P, (c + 1) * P)
                yield w_small[:, :, c, :], [(a["gate"][rows, :], 0, P, 0, EXPERTS), (a["router"][rows, :], 0, P, ROUTER_AT, A_AT),
                                            (a["A"][rows, :], 0, P, A_AT, W_SMALL)]
            yield w_b[:, :, :], [(a["B"], 0, 64, 0, 512), (a["B"], 64, P, 0, 512)]
            yield bias_e[:, :, :], [(a["expert_b"], 0, EXPERTS, 0, 512)]

        work = list(pieces())
        N = len(work)
        landed = [0] * len(slots)
        landed_by = []
        for i, (_, parts) in enumerate(work):
            landed[i % len(slots)] += 16 * len(parts)
            landed_by.append(landed[i % len(slots)])

        def staged(i):
            return s[f"staged{i % len(slots)}"]

        def piece(i):
            dst, parts = work[i]
            n = parts[-1][2] if len(parts) > 1 else parts[0][2]
            return dst, slots[i % len(slots)][0:n, 0:parts[-1][4]]

        @block.sync
        def _(sp):
            for dst, src in ((ident32, "ident"), (rope0, "rope0"), (cos1, "cos1"), (sin1, "sin1"), (iota8, "iota8")):
                sp.dma_start(dst[:], a[src]).then_inc(s["const"], 16)
            for dst, src in ((bias_qkv1, "b_qkv1"), (bias_o1, "b_o1"), (gate_bias, "gate_b")):
                sp.dma_start(dst[:], a[src].partition_broadcast(P)).then_inc(s["const"], 16)
            for i, (_, parts) in enumerate(work):
                if i >= len(slots):
                    sp.wait_ge(s["w_hi"], i - len(slots) + 1)
                    sp.wait_ge(s["w_lo"], i - len(slots) + 1)
                for src, p0, p1, c0, c1 in parts:
                    sp.dma_start(slots[i % len(slots)][p0:p1, c0:c1], src).then_inc(staged(i), 16)
            with sp.Fori(0, BATCH) as b:
                sp.wait_ge(s["x_out"], b * 16)
                sp.dma_start(x[:], a["x"][bass.ds(b, 1)].rearrange("b (t p) c -> p (b t) c", p=P)).then_inc(s["x_in"], 16)
                sp.wait_ge(s["resid"], b * 4 + 4)
                sp.dma_start(a["out"][bass.ds(b, 1)].rearrange("b (t p) c -> p (b t) c", p=P), x[:]).then_inc(s["x_out"], 16)
            sp.wait_ge(s["x_out"], BATCH * 16)

        @block.gpsimd
        def _(pool):
            pool.memset(mask_qk[:], 0.0).then_inc(s["masks"], 1)
            pool.memset(mask_kq[:], 0.0).then_inc(s["masks"], 1)
            pool.memset(minus_half[:], -0.5).then_inc(s["masks"], 1)
            pool.wait_ge(s["masks"], 3)
            pool.affine_select(out=mask_qk[:], in_=mask_qk[:], compare_op=ALU.is_ge, fill=NEG, base=0,
                               pattern=[[0, GROUP], [-1, P]], channel_multiplier=1).then_inc(s["masks"], 1)
            pool.affine_select(out=mask_kq[:], in_=mask_kq[:], compare_op=ALU.is_ge, fill=NEG, base=0,
                               pattern=[[0, GROUP], [1, P]], channel_multiplier=-1).then_inc(s["masks"], 1)
            pool.wait_ge(s["w_hi"], N)
            pool.wait_ge(s["w_lo"], N)
            for half, at in ((qs, None), (ks0, 1.0)):
                for t in range(TILES):
                    pool.memset(half[:, t, :, MAXROW:MAXROW + 2], 0.0 if at is None else at)
                    last = pool.memset(half[:, t, :, MAXROW + 2:BLK], 0.0)
            last.then_inc(s["cleared"], 1)

            def rms(b, l):
                pool.wait_ge(s["var"], b * 2 + l + 1)
                pool.tensor_tensor(rstd[:], var_eps[:], minus_half[:], ALU.pow).then_inc(s["rstd"], 1)

            def split_qk(b, l, t):
                pool.wait_ge(s["qk_hi"], 4 * b + 2 * l + t + 1)
                q = qk[:, 0:512].rearrange("p (h d) -> p h d", d=HD)
                pool.tensor_tensor(qs[:, t, :, HD:2 * HD], q, qs[:, t, :, 0:HD], ALU.subtract)
                pool.memset(qs[:, t, :, MAXROW:MAXROW + 2], 0.0)
                if l == 0:
                    k = qk[:, 512:1024].rearrange("p (h d) -> p h d", d=HD)
                    last = pool.tensor_tensor(ks0[:, t, :, 2 * HD:3 * HD], k, ks0[:, t, :, 0:HD], ALU.subtract)
                else:
                    k = qk[:, 512:640].rearrange("p (h d) -> p h d", d=HD)
                    for j in range(2):
                        dst = ks1[:, t, j::2, :]
                        last = pool.tensor_tensor(dst[:, :, 2 * HD:3 * HD], k, dst[:, :, 0:HD], ALU.subtract)
                last.then_inc(s["qk_lo"], 1)

            with pool.Fori(0, BATCH) as b:
                for l in range(2):
                    rms(b, l)
                    for t in range(TILES):
                        split_qk(b, l, t)
                    for g in range(GROUPS):
                        n = b * 16 + (8 * l + g)
                        pool.wait_ge(s["p_hi"], n + 1)
                        pool.wait_ge(s["pv"], n)
                        pool.tensor_tensor(p_lo[:], p32[:], p_hi[:], ALU.subtract).then_inc(s["p_lo"], 1)

        @block.scalar
        def _(act):
            for i in range(N):
                act.wait_ge(staged(i), landed_by[i])
                dst, src = piece(i)
                act.activation(dst[:, 0, :], src, ACT.Copy, scale=WS).then_inc(s["w_hi"], 1)
            act.wait_ge(s["const"], 8 * 16)
            act.wait_ge(s["cleared"], 1)

            def turned(b, l, src_sem, dst_sem, used_sem, dst):
                for t in range(TILES):
                    act.wait_ge(s[src_sem], 4 * b + 2 * l + t + 1)
                    act.activation(dst[:, 0, :, t * P:(t + 1) * P], psA[:, t, :].rearrange("p (c n) -> p c n", c=CH),
                                   ACT.Copy, scale=XS).then_inc(s[dst_sem], 1)

            def heads_hi(b, l, t):
                m = 4 * b + 2 * l + t
                act.wait_ge(s["rope"], m + 1)
                q = qk[:, 0:512].rearrange("p (h d) -> p h d", d=HD)
                if l == 0:
                    act.activation(vs[:, t, :, 0:HD], qkv_ps[t][:, 2, :].rearrange("p (h d) -> p h d", d=HD),
                                   ACT.Copy, scale=OUT)
                    k = qk[:, 512:1024].rearrange("p (h d) -> p h d", d=HD)
                    for j in range(2):
                        act.activation(ks0[:, t, :, j * HD:(j + 1) * HD], k, ACT.Copy)
                else:
                    act.activation(vs[:, t, 0:KV_HEADS, 0:HD], qkv1[:, 640:768].rearrange("p (h d) -> p h d", d=HD),
                                   ACT.Copy)
                    k = qk[:, 512:640].rearrange("p (h d) -> p h d", d=HD)
                    for j in range(2):
                        for i in range(2):
                            act.activation(ks1[:, t, j::2, i * HD:(i + 1) * HD], k, ACT.Copy)
                for j in (2, 0):
                    last = act.activation(qs[:, t, :, j * HD:(j + 1) * HD], q, ACT.Copy)
                last.then_inc(s["qk_hi"], 1)

            def group(b, l, g):
                n = b * 16 + (8 * l + g)
                act.wait_ge(s["t1"], n + 1)
                act.activation(qT[:], tA[:, 0:PAIRS * SEQ].rearrange("p (j n) -> p j n", j=PAIRS), ACT.Copy).then_inc(s["q_t"], 1)
                act.wait_ge(s["t2"], n + 1)
                act.activation(qmT[:], tA[:, 0:PAIRS * SEQ].rearrange("p (j n) -> p j n", j=PAIRS), ACT.Copy).then_inc(s["qm_t"], 1)
                act.wait_ge(s["st"], n + 1)
                act.wait_ge(s["p_lo"], n)
                scale = HD ** -0.5 if l == 0 else 1.0 / HD
                src = psB[:].rearrange("p a n -> p (a n)")
                act.activation(p32[:], src, ACT.Exp, scale=scale).then_inc(s["p32"], 1)
                act.wait_ge(s["pv"], n)
                act.activation(p_hi[:], src, ACT.Exp, scale=scale).then_inc(s["p_hi"], 1)

            with act.Fori(0, BATCH) as b:
                turned(b, 0, "xt_ps", "xt_hi", None, xT)
                for t in range(TILES):
                    act.wait_ge(s["proj"], 4 * b + t + 1)
                    act.wait_ge(s["rope"], 4 * b + t)
                    src = qkv_ps[t][:, 0:2, :].rearrange("p a (n two) -> p (a n) two", two=2)
                    dst = rot[:].rearrange("p (n two) -> p n two", two=2)
                    act.activation(dst[:, :, 0], src[:, :, 1], ACT.Copy, scale=rope0[:, t, 1:2])
                    act.activation(dst[:, :, 1], src[:, :, 0], ACT.Copy, scale=rope0[:, t, 2:3]).then_inc(s["rot"], 1)
                    heads_hi(b, 0, t)
                act.wait_ge(s["chosen_T"], b + 1)
                act.activation(chosenT[:], tW[0:EXPERTS, 0:SEQ], ACT.Copy, scale=XS).then_inc(s["chosenT"], 1)
                for t in range(TILES):
                    act.wait_ge(s["ffn_bias"], 2 * b + t + 1)
                    act.activation(ffn[:, t, :], psW[:], ACT.Copy).then_inc(s["ffn_in"], 1)
                for g in range(GROUPS):
                    group(b, 0, g)
                turned(b, 0, "at_ps", "at_hi", None, aT)
                act.wait_ge(s["mixed"], b * 16 + 16)
                for t in range(TILES):
                    act.activation(th[:, t, :], ffn[:, t, :], ACT.Tanh, scale=0.5 * OUT).then_inc(s["th"], 1)
                turned(b, 1, "xt_ps", "xt_hi", None, xT)
                act.wait_ge(s["r_bias"], b + 1)
                for t in range(TILES):
                    last = act.activation(r_exp[:, t, :], logits[:, t, 0:LORA], ACT.Exp, bias=r_bias[:, t:t + 1])
                last.then_inc(s["r_exp"], 1)
                for t in range(TILES):
                    heads_hi(b, 1, t)
                for g in range(GROUPS):
                    group(b, 1, g)
                act.wait_ge(s["mid_ps"], b + 1)
                act.activation(midT[:], tW[:, 0:SEQ], ACT.Copy).then_inc(s["midT"], 1)
                turned(b, 1, "at_ps", "at_hi", None, aT)
                for t in range(TILES):
                    act.wait_ge(s["delta"], 2 * b + t + 1)
                    act.activation(ffn[:, t, :], delta_ps[t], ACT.Copy, scale=OUT).then_inc(s["ffn1"], 1)
                act.wait_ge(s["ffn1"], 2 * b + 2)
                for t in range(TILES):
                    act.activation(th[:, t, :], ffn[:, t, :], ACT.Tanh, scale=0.5).then_inc(s["th"], 1)

        @block.vector
        def _(dve):
            for i in range(N):
                dst, src = piece(i)
                dve.wait_ge(staged(i), landed_by[i])
                dve.wait_ge(s["w_hi"], i + 1)
                dve.scalar_tensor_tensor(out=dst[:, 1, :], in0=src, scalar=WS, in1=dst[:, 0, :],
                                         op0=ALU.mult, op1=ALU.subtract).then_inc(s["w_lo"], 1)
            dve.wait_ge(s["w_lo"], N)
            dve.memset(w_b[64:P, 1, :], 0.0)
            dve.memset(vs[:, :, :, HD:HD + 1], 1.0)
            dve.memset(kT[64:P, :, 0, :], 0.0)
            dve.memset(kT[0:64, :, 1, :], 0.0)
            dve.wait_ge(s["const"], 8 * 16)
            dve.tensor_copy(ident16[:], ident32[:])
            dve.tensor_copy(identb[:], ident32[:]).then_inc(s["made"], 1)

            def wait_alone(name, value):
                value = dve.snap(value)
                dve.wait_ge(s["const"], 8 * 16)
                dve.wait_ge(s[name], value)

            def norm(b, l):
                m = 2 * b + l
                if l == 0:
                    dve.wait_ge(s["x_in"], 16 * b + 16)
                else:
                    dve.wait_ge(s["resid"], 4 * b + 2)
                for t in range(TILES):
                    dve.bn_stats(stats[:, t, :], x[:, t, :]).then_inc(s["bn"], 1)
                dve.wait_ge(s["bn"], 2 * m + 2)
                dve.memset(var_eps[:], EPS)
                for t in range(TILES):
                    dve.bn_aggr(mv[:, t, :], stats[:, t, :]).then_inc(s["mv"], 1)
                dve.wait_ge(s["mv"], 2 * m + 2)
                dve.tensor_tensor(var_eps[:], mv[:, :, 1], var_eps[:], ALU.add).then_inc(s["var"], 1)
                dve.wait_ge(s["rstd"], m + 1)
                for t in range(TILES):
                    dve.tensor_scalar(xn[:, t, :], x[:, t, :], mv[:, t, 0:1], rstd[:, t:t + 1],
                                      ALU.subtract, ALU.mult).then_inc(s["xn"], 1)

            def turned(b, l, hi_sem, lo_sem, dst):
                for t in range(TILES):
                    dve.wait_ge(s[hi_sem], 4 * b + 2 * l + t + 1)
                    at = slice(t * P, (t + 1) * P)
                    dve.scalar_tensor_tensor(out=dst[:, 1, :, at], in0=psA[:, t, :].rearrange("p (c n) -> p c n", c=CH),
                                             scalar=XS, in1=dst[:, 0, :, at], op0=ALU.mult, op1=ALU.subtract).then_inc(s[lo_sem], 1)

            def group(b, l, g):
                n = b * 16 + (8 * l + g)
                dve.wait_ge(s["q_t"], n + 1)
                k = tA[:, PAIRS * SEQ:2 * PAIRS * SEQ].rearrange("p (j n) -> p j n", j=PAIRS)
                w = PAIRS if l == 0 else 1
                dve.tensor_copy(kT[0:64, 0:w, 0, :], k[0:64, 0:w, :])
                dve.tensor_copy(kT[64:P, 0:w, 1, :], k[64:P, 0:w, :]).then_inc(s["k_t"], 1)
                dve.wait_ge(s["s_ps"], n + 1)
                dve.tensor_reduce(neg_max[:, 0, :], psA[:, 0, :].rearrange("p (h k) -> p h k", h=GROUP), AX.X, ALU.max, negate=True)
                dve.tensor_reduce(neg_max[:, 1, :], psA[:, 1:3, :].rearrange("p a (h k) -> p (a h) k", h=PAIRS), AX.X, ALU.max,
                                  negate=True).then_inc(s["neg_max"], 1)
                dve.wait_ge(s["neg_max"], n + 1)
                hi = qs[:, :, GROUP * g:GROUP * (g + 1), MAXROW]
                dve.tensor_copy(hi, neg_max[:]).then_inc(s["max_hi"], 1)
                dve.wait_ge(s["max_hi"], n + 1)
                dve.tensor_tensor(qs[:, :, GROUP * g:GROUP * (g + 1), MAXROW + 1], neg_max[:], hi, ALU.subtract).then_inc(s["max_lo"], 1)

            def outputs(b, l, g):
                n = b * 16 + (8 * l + g)
                dve.wait_ge(s["pv"], n + 1)
                dve.reciprocal(recip[:], o_ps[:, :, :, HD])
                dve.tensor_copy(o_lo[:], o_ps[:, :, :, HD + 1:VW]).then_inc(s["o_lo"], 1)
                dve.wait_ge(s["o_lo"], n + 1)
                dve.tensor_tensor(o_sum[:], o_ps[:, :, :, 0:HD], o_lo[:], ALU.add).then_inc(s["o_sum"], 1)
                dve.wait_ge(s["o_sum"], n + 1)
                dst = attn[:].rearrange("p t (h d) -> p t h d", d=HD)[:, :, GROUP * g:GROUP * (g + 1), :]
                dve.tensor_tensor(dst, o_sum[:], recip[:].unsqueeze(3).broadcast_to([P, TILES, GROUP, HD]), ALU.mult).then_inc(s["attn"], 1)

            def expert(b, e, t):
                n = b * 16 + (2 * e + t)
                dve.wait_ge(s["expert"], n + 1)
                if e:
                    dve.wait_ge(s["mixed"], n - 1)
                dve.scalar_tensor_tensor(out=ffn[:, t, :], in0=psW[:], scalar=chosen[:, t, e:e + 1], in1=ffn[:, t, :],
                                         op0=ALU.mult, op1=ALU.add).then_inc(s["mixed"], 1)

            with dve.Fori(0, BATCH) as b:
                norm(b, 0)
                turned(b, 0, "xt_hi", "xt_lo", xT)
                for t in range(TILES):
                    m = 4 * b + t
                    dve.wait_ge(s["qk_lo"], m)
                    dve.wait_ge(s["rot"], 2 * b + t + 1)
                    dve.scalar_tensor_tensor(out=qk[:], in0=qkv_ps[t][:, 0:2, :].rearrange("p a n -> p (a n)"), scalar=rope0[:, t, 0:1],
                                             in1=rot[:], op0=ALU.mult, op1=ALU.add).then_inc(s["rope"], 1)
                    dve.wait_ge(s["qk_hi"], m + 1)
                    dve.scalar_tensor_tensor(out=vs[:, t, :, HD + 1:VW], in0=qkv_ps[t][:, 2, :].rearrange("p (h d) -> p h d", d=HD),
                                             scalar=OUT, in1=vs[:, t, :, 0:HD], op0=ALU.mult, op1=ALU.subtract).then_inc(s["v_lo"], 1)
                dve.wait_ge(s["small"], 2 * b + 1)
                for t in range(TILES):
                    dve.scalar_tensor_tensor(out=logits[:, t, :], in0=psW[:, W_SMALL * t:W_SMALL * t + EXPERTS], scalar=OUT,
                                             in1=gate_bias[:], op0=ALU.mult, op1=ALU.add).then_inc(s["logits"], 1)
                wait_alone("logits", 4 * b + 2)
                for t in range(TILES):
                    dve.max(top[:, t, :], logits[:, t, :]).then_inc(s["top"], 1)
                wait_alone("top", 4 * b + 2)
                for t in range(TILES):
                    dve.max_index(top_at[:, t, :], top[:, t, :], logits[:, t, :]).then_inc(s["top_at"], 1)
                dve.wait_ge(s["top_at"], 4 * b + 2)
                dve.tensor_copy(top_f[:], top_at[:, :, 0:2]).then_inc(s["top_f"], 1)
                dve.wait_ge(s["top_f"], 2 * b + 1)
                for t in range(TILES):
                    dve.tensor_scalar(chosen[:, t, :], iota8[:], top_f[:, t, 0:1], None, ALU.is_equal)
                    last = dve.tensor_scalar(chosen16[:, t, :], iota8[:], top_f[:, t, 0:1], None, ALU.is_equal)
                last.then_inc(s["chosen"], 1)
                dve.wait_ge(s["ffn_in"], 2 * b + 2)
                for g in range(GROUPS):
                    group(b, 0, g)
                    expert(b, g, 0)
                    if g:
                        outputs(b, 0, g - 1)
                    expert(b, g, 1)
                outputs(b, 0, GROUPS - 1)
                turned(b, 0, "at_hi", "at_lo", aT)
                for t in range(TILES):
                    m = 4 * b + t
                    dve.wait_ge(s["th"], m + 1)
                    dve.scalar_tensor_tensor(out=th[:, t, :], in0=th[:, t, :], scalar=1.0, in1=ffn[:, t, :],
                                             op0=ALU.add, op1=ALU.mult).then_inc(s["gated"], 1)
                    dve.wait_ge(s["gated"], m + 1)
                    dve.wait_ge(s["out"], m + 1)
                    dve.scalar_tensor_tensor(out=th[:, t, :], in0=psB[:, t, :], scalar=0.5 * OUT * OUT, in1=th[:, t, :],
                                             op0=ALU.mult, op1=ALU.mult).then_inc(s["weighed"], 1)
                    dve.wait_ge(s["weighed"], m + 1)
                    dve.tensor_tensor(x[:, t, :], x[:, t, :], th[:, t, :], ALU.add).then_inc(s["resid"], 1)
                norm(b, 1)
                turned(b, 1, "xt_hi", "xt_lo", xT)
                dve.wait_ge(s["small"], 2 * b + 2)
                for t in range(TILES):
                    at = W_SMALL * t
                    dve.memset(logits[:, t, LORA:8], NEG)
                    dve.tensor_scalar(logits[:, t, 0:LORA], psW[:, at + ROUTER_AT:at + A_AT], OUT, None, ALU.mult).then_inc(s["logits"], 1)
                wait_alone("logits", 4 * b + 4)
                for t in range(TILES):
                    dve.max(top[:, t, :], logits[:, t, :]).then_inc(s["top"], 1)
                dve.wait_ge(s["top"], 4 * b + 4)
                dve.tensor_scalar(r_bias[:], top[:, :, 0], -1.0, None, ALU.mult).then_inc(s["r_bias"], 1)
                for t in range(TILES):
                    dve.max_index(top_at[:, t, :], top[:, t, :], logits[:, t, :]).then_inc(s["top_at"], 1)
                dve.wait_ge(s["top_at"], 4 * b + 4)
                dve.tensor_copy(top_f[:], top_at[:, :, 0:2]).then_inc(s["top_f"], 1)
                dve.wait_ge(s["top_f"], 2 * b + 2)
                for t in range(TILES):
                    dve.tensor_scalar(r_sel[:, t, :], iota8[:, 0:LORA], top_f[:, t, 0:1], None, ALU.is_equal).then_inc(s["r_first"], 1)
                dve.wait_ge(s["r_first"], 2 * b + 2)
                for t in range(TILES):
                    dve.scalar_tensor_tensor(out=r_sel[:, t, :], in0=iota8[:, 0:LORA], scalar=top_f[:, t, 1:2], in1=r_sel[:, t, :],
                                             op0=ALU.is_equal, op1=ALU.add).then_inc(s["r_sel"], 1)
                dve.wait_ge(s["r_sel"], 2 * b + 2)
                dve.wait_ge(s["r_exp"], b + 1)
                dve.tensor_tensor(r_exp[:], r_exp[:], r_sel[:], ALU.mult).then_inc(s["r_eg"], 1)
                dve.wait_ge(s["r_eg"], b + 1)
                dve.tensor_reduce(r_sum[:], r_exp[:], AX.X, ALU.add).then_inc(s["r_sum"], 1)
                dve.wait_ge(s["r_sum"], b + 1)
                dve.reciprocal(r_rec[:], r_sum[:]).then_inc(s["r_rec"], 1)
                dve.wait_ge(s["r_rec"], b + 1)
                for t in range(TILES):
                    dve.tensor_scalar(r_gate[:, t, :], r_exp[:, t, :], r_rec[:, t:t + 1], LORA_SCALE * OUT * XS,
                                      ALU.mult, ALU.mult).then_inc(s["r_gate"], 1)
                dve.wait_ge(s["r_gate"], 2 * b + 2)
                for t in range(TILES):
                    at = W_SMALL * t + A_AT
                    dve.tensor_tensor(mid[:, t, :].rearrange("p (e r) -> p e r", e=LORA),
                                      psW[:, at:at + LORA * RANK].rearrange("p (e r) -> p e r", e=LORA),
                                      r_gate[:, t, :].unsqueeze(2).broadcast_to([P, LORA, RANK]), ALU.mult).then_inc(s["mid"], 1)
                dve.wait_ge(s["mid"], 2 * b + 2)
                dve.tensor_copy(mid16[:, :, 0, :], mid[:]).then_inc(s["mid_hi"], 1)
                dve.wait_ge(s["mid_hi"], b + 1)
                dve.tensor_tensor(mid16[:, :, 1, :], mid[:], mid16[:, :, 0, :], ALU.subtract).then_inc(s["mid_lo"], 1)
                for t in range(TILES):
                    m = 4 * b + 2 + t
                    dve.wait_ge(s["proj"], m + 1)
                    dve.wait_ge(s["qk_lo"], m)
                    dve.wait_ge(s["v_lo"], m)
                    for lo, hi, bank in ((0, 512, 0), (512, 768, 1)):
                        last = dve.scalar_tensor_tensor(out=qkv1[:, lo:hi], in0=qkv_ps[t][:, bank, 0:hi - lo], scalar=OUT,
                                                        in1=bias_qkv1[:, lo:hi], op0=ALU.mult, op1=ALU.add)
                    last.then_inc(s["qkv1"], 1)
                    dve.wait_ge(s["qkv1"], 2 * b + t + 1)
                    src = qkv1[:, 0:640].rearrange("p (h d) -> p h d", d=HD)
                    dst = rot[:, 0:640].rearrange("p (h d) -> p h d", d=HD)
                    half = HD // 2
                    n_h = HEADS + KV_HEADS
                    for lo in (0, half):
                        hi = half - lo
                        dve.tensor_tensor(dst[:, :, lo:lo + half], src[:, :, hi:hi + half],
                                          sin1[:, t, lo:lo + half].unsqueeze(1).broadcast_to([P, n_h, half]), ALU.mult)
                    dve.tensor_tensor(qk[:, 0:640].rearrange("p (h d) -> p h d", d=HD), src,
                                      cos1[:, t, :].unsqueeze(1).broadcast_to([P, n_h, HD]), ALU.mult).then_inc(s["cosx"], 1)
                    dve.wait_ge(s["cosx"], 2 * b + t + 1)
                    dve.tensor_tensor(qk[:, 0:640], qk[:, 0:640], rot[:, 0:640], ALU.add).then_inc(s["rope"], 1)
                    dve.wait_ge(s["qk_hi"], m + 1)
                    dve.tensor_tensor(vs[:, t, 0:KV_HEADS, HD + 1:VW], qkv1[:, 640:768].rearrange("p (h d) -> p h d", d=HD),
                                      vs[:, t, 0:KV_HEADS, 0:HD], ALU.subtract).then_inc(s["v_lo"], 1)
                for g in range(GROUPS):
                    group(b, 1, g)
                    if g:
                        outputs(b, 1, g - 1)
                outputs(b, 1, GROUPS - 1)
                turned(b, 1, "at_hi", "at_lo", aT)
                for t in range(TILES):
                    m = 4 * b + 2 + t
                    dve.wait_ge(s["th"], m + 1)
                    dve.scalar_tensor_tensor(out=th[:, t, :], in0=th[:, t, :], scalar=1.0, in1=ffn[:, t, :],
                                             op0=ALU.add, op1=ALU.mult).then_inc(s["gated"], 1)
                    dve.wait_ge(s["out"], m + 1)
                    dve.scalar_tensor_tensor(out=attn[:, t, :], in0=psB[:, t, :], scalar=OUT, in1=bias_o1[:],
                                             op0=ALU.mult, op1=ALU.add).then_inc(s["s1"], 1)
                    dve.wait_ge(s["gated"], m + 1)
                    dve.wait_ge(s["s1"], 2 * b + t + 1)
                    dve.scalar_tensor_tensor(out=th[:, t, :], in0=attn[:, t, :], scalar=0.5, in1=th[:, t, :],
                                             op0=ALU.mult, op1=ALU.mult).then_inc(s["weighed"], 1)
                    dve.wait_ge(s["weighed"], m + 1)
                    dve.tensor_tensor(x[:, t, :], x[:, t, :], th[:, t, :], ALU.add).then_inc(s["resid"], 1)

        @block.tensor
        def _(pe):
            pe.wait_ge(s["made"], 1)
            pe.wait_ge(s["cleared"], 1)
            pe.wait_ge(s["masks"], 5)
            pe.wait_ge(s["w_hi"], N)
            pe.wait_ge(s["w_lo"], N)

            def product(outs, lhs, t, rhs):
                at = slice(t * P, (t + 1) * P)
                steps = [(c, i, j) for c in range(CH) for i, j in ((0, 0), (0, 1), (1, 0))]
                for c, i, j in steps:
                    for out, (w, lo, hi) in zip(outs, rhs):
                        last = pe.matmul(out, lhs[:, i, c, at], w[:, j, c, lo:hi], start=(c, i, j) == steps[0],
                                         stop=(c, i, j) == steps[-1])
                return last

            def turn(src, m, ready, done):
                for t in range(TILES):
                    ready(t)
                    for c in range(CH):
                        last = pe.transpose(psA[:, t, c * P:(c + 1) * P], src[:, t, c * P:(c + 1) * P], ident32[:])
                    last.then_inc(s[done], 1)

            def stack_turns(g, l, q_only):
                for j in range(PAIRS):
                    for t in range(TILES):
                        h = GROUP * g + 2 * j
                        last = pe.transpose(tA[:, j * SEQ + t * P:j * SEQ + (t + 1) * P],
                                            qs[:, t, h:h + 2, :].rearrange("p h k -> p (h k)"), ident16[:])
                if not q_only:
                    for j in range(PAIRS if l == 0 else 1):
                        for t in range(TILES):
                            k = ks0[:, t, GROUP * g + 2 * j:GROUP * g + 2 * j + 2, :] if l == 0 else ks1[:, t, 2 * g:2 * g + 2, :]
                            at = PAIRS * SEQ + j * SEQ + t * P
                            last = pe.transpose(tA[:, at:at + P], k.rearrange("p h k -> p (h k)"), ident16[:])
                return last

            def scores(l):
                pe.matmul(psA[:, 0, :], identb[:], mask_qk[:].rearrange("p h k -> p (h k)"), start=True, stop=False, skip_group_check=True)
                for j in range(PAIRS):
                    kj = j if l == 0 else 0
                    pe.matmul(psA[:, 0, 2 * P * j:2 * P * (j + 1)].rearrange("p (h k) -> p h k", h=2), qT[:, j, 0:P], kT[:, kj, :, 0:P],
                              start=False, stop=True, skip_group_check=True)
                for j in range(PAIRS):
                    kj = j if l == 0 else 0
                    pe.matmul(psA[:, 1 + j, :].rearrange("p (h k) -> p h k", h=2)[:, :, P:SEQ], identb[:], mask_qk[:, 0:2, :],
                              start=True, stop=False, skip_group_check=True)
                    last = pe.matmul(psA[:, 1 + j, :].rearrange("p (h k) -> p h k", h=2), qT[:, j, P:SEQ], kT[:, kj, :, :],
                                     start=False, stop=True, skip_group_check=True)
                return last

            def scores_t(l):
                for j in range(PAIRS):
                    kj = j if l == 0 else 0
                    out = psB[:, j, :].rearrange("p (h q) -> p h q", h=2)
                    pe.matmul(out[:, :, 0:P], identb[:], mask_kq[:, 0:2, :], start=True, stop=False, skip_group_check=True)
                    for h in range(2):
                        pe.matmul(out[:, h, :], kT[:, kj, h, 0:P], qmT[:, j, :], start=False, stop=True, skip_group_check=True)
                pe.matmul(psB[:, 2, :], identb[:], mask_kq[:].rearrange("p h k -> p (h k)"), start=True, stop=False, skip_group_check=True)
                for j in range(PAIRS):
                    kj = j if l == 0 else 0
                    for h in range(2):
                        last = pe.matmul(psB[:, 2, P * (2 * j + h):P * (2 * j + h + 1)], kT[:, kj, h, P:SEQ], qmT[:, j, P:SEQ],
                                         start=False, stop=True, skip_group_check=True)
                return last

            def values(g, l):
                for h in range(GROUP):
                    v = GROUP * g + h if l == 0 else g
                    for t in range(TILES):
                        for k in range(t + 1):
                            at = SEQ * h + P * t if k == 0 else GROUP * SEQ + P * h
                            pe.matmul(o_ps[:, t, h, :], p_hi[:, at:at + P], vs[:, k, v, :], start=k == 0, stop=False, skip_group_check=True)
                            last = pe.matmul(o_ps[:, t, h, 0:HD + 1], p_lo[:, at:at + P], vs[:, k, v, 0:HD + 1], start=False,
                                             stop=k == t, skip_group_check=True)
                return last

            def expert(b, e, t):
                n = b * 16 + (2 * e + t)
                pe.wait_ge(s["mixed"], n)
                product([psW[:]], xT, t, [(w_exp, 512 * e, 512 * (e + 1))]).then_inc(s["expert"], 1)

            def attention(b, l):
                for g in range(GROUPS):
                    n = b * 16 + (8 * l + g)
                    pe.wait_ge(s["qm_t"], n)
                    if g == 0:
                        pe.wait_ge(s["qk_lo"], 4 * b + 2 * l + 2)
                        pe.wait_ge(s["v_lo"], 4 * b + 2 * l + 2)
                    stack_turns(g, l, False).then_inc(s["t1"], 1)
                    pe.wait_ge(s["q_t"], n + 1)
                    pe.wait_ge(s["k_t"], n + 1)
                    scores(l).then_inc(s["s_ps"], 1)
                    if l == 0:
                        expert(b, g, 0)
                    pe.wait_ge(s["max_lo"], n + 1)
                    stack_turns(g, l, True).then_inc(s["t2"], 1)
                    if g:
                        pe.wait_ge(s["p_lo"], n)
                        if g > 1:
                            pe.wait_ge(s["attn"], n - 1)
                        values(g - 1, l).then_inc(s["pv"], 1)
                    pe.wait_ge(s["qm_t"], n + 1)
                    pe.wait_ge(s["p_hi"], n)
                    scores_t(l).then_inc(s["st"], 1)
                    if l == 0:
                        expert(b, g, 1)
                n = b * 16 + 8 * (l + 1)
                pe.wait_ge(s["p_lo"], n)
                pe.wait_ge(s["attn"], n - 1)
                values(GROUPS - 1, l).then_inc(s["pv"], 1)

            with pe.Fori(0, BATCH) as b:
                for l in range(2):
                    m = 4 * b + 2 * l

                    def normed(t):
                        pe.wait_ge(s["xn"], m + t + 1)
                        pe.wait_ge(s["at_lo"], m)

                    turn(xn, m, normed, "xt_ps")
                    for t in range(TILES):
                        pe.wait_ge(s["xt_lo"], m + t + 1)
                        if t == 0:
                            pe.wait_ge(s["resid"], m)
                            if l == 0:
                                pe.wait_ge(s["ffn1"], 2 * b)
                        else:
                            pe.wait_ge(s["xt_lo"], m + 2)
                        at = W_SMALL * t
                        small = product([psW[:, at:at + W_SMALL]], xT, t, [(w_small, 0, W_SMALL)])
                        if t == 1:
                            small.then_inc(s["small"], 1)
                        if l == 0:
                            product([qkv_ps[t][:, i, :] for i in range(3)], xT, t,
                                    [(w_qkv0, 512 * i, 512 * (i + 1)) for i in range(3)]).then_inc(s["proj"], 1)
                        else:
                            product([qkv_ps[t][:, 0, :], qkv_ps[t][:, 1, 0:256]], xT, t,
                                    [(w_qkv1, 0, 512), (w_qkv1, 512, 768)]).then_inc(s["proj"], 1)
                    if l == 0:
                        pe.wait_ge(s["chosen"], b + 1)
                        for t in range(TILES):
                            last = pe.transpose(tW[0:EXPERTS, t * P:(t + 1) * P], chosen16[:, t, :], ident16[:])
                        last.then_inc(s["chosen_T"], 1)
                        pe.wait_ge(s["chosenT"], b + 1)
                        for t in range(TILES):
                            pe.wait_ge(s["ffn_in"], 2 * b + t)
                            for j in range(2):
                                last = pe.matmul(psW[:], chosenT[:, t * P:(t + 1) * P], bias_e[:, j, :], start=j == 0, stop=j == 1)
                            last.then_inc(s["ffn_bias"], 1)
                        pe.wait_ge(s["ffn_in"], 2 * b + 2)
                    attention(b, l)
                    if l == 1:
                        pe.wait_ge(s["mid_lo"], b + 1)
                        for t in range(TILES):
                            last = pe.transpose(tW[:, t * P:(t + 1) * P], mid16[:, t, :, :].rearrange("p a n -> p (a n)"), ident16[:])
                        last.then_inc(s["mid_ps"], 1)

                    def attended(t):
                        pe.wait_ge(s["attn"], b * 16 + 8 * (l + 1))

                    turn(attn, m, attended, "at_ps")
                    if l == 1:
                        pe.wait_ge(s["midT"], b + 1)
                        for t in range(TILES):
                            for j in range(2):
                                last = pe.matmul(delta_ps[t], midT[:, t * P:(t + 1) * P], w_b[:, j, :], start=j == 0, stop=j == 1)
                            last.then_inc(s["delta"], 1)
                    for t in range(TILES):
                        pe.wait_ge(s["at_lo"], m + t + 1)
                        pe.wait_ge(s["p_hi"], b * 16 + 8 * (l + 1))
                        product([psB[:, t, :]], aT, t, [((w_o0, w_o1)[l], 0, 512)]).then_inc(s["out"], 1)


_OUT = (BATCH, SEQ, C)


def kernel(**inputs):
    import concourse.bacc as _bacc
    from concourse.bass_utils import run_bass_kernel_spmd as _run

    v = {k: np.asarray(w) for k, w in inputs.items()}
    rows = np.arange(W_QKV1).reshape(KV_HEADS, GROUP + 2, HD)
    order = np.concatenate([rows[:, :GROUP].ravel(), rows[:, GROUP].ravel(), rows[:, GROUP + 1].ravel()])
    t = np.arange(SEQ, dtype=np.float32)
    inv = (1.0 / 1000000.0 ** (np.arange(0, HD, 2, dtype=np.float32) / HD)).astype(np.float32)
    freq = np.outer(t, inv).astype(np.float32)

    def tiled(table):
        return np.ascontiguousarray(table.reshape(TILES, P, -1).transpose(1, 0, 2)).astype(np.float32)

    arrays = {
        "x": v["L0_attn_x"],
        "wqkv0": np.concatenate([v["L0_attn_wq"].T, v["L0_attn_wk"].T, v["L0_attn_wv"].T], axis=1),
        "wo0": v["L0_attn_wo"].T,
        "gate": v["L0_ffn_gate_w"].T,
        "gate_b": v["L0_ffn_gate_b"],
        "wexp": v["L0_ffn_expert_w"].reshape(-1, C).T,
        "expert_b": v["L0_ffn_expert_b"],
        "wqkv1": v["L1_attn_w_qkv"][order].T,
        "b_qkv1": v["L1_attn_b_qkv"][order],
        "wo1": v["L1_attn_w_dense"].T,
        "b_o1": v["L1_attn_b_dense"],
        "router": v["L1_ffn_router_w"].T,
        "A": v["L1_ffn_A"].reshape(-1, C).T,
        "B": v["L1_ffn_B"].transpose(0, 2, 1).reshape(-1, C),
        "ident": np.eye(P, dtype=np.float32),
        "rope0": tiled(np.stack([np.cos(t) * OUT, -np.sin(t) * OUT, np.sin(t) * OUT], axis=1)),
        "cos1": tiled(np.concatenate([np.cos(freq), np.cos(freq)], axis=1)),
        "sin1": tiled(np.concatenate([-np.sin(freq), np.sin(freq)], axis=1)),
        "iota8": np.tile(np.arange(8, dtype=np.float32), (P, 1)),
    }
    nc = _bacc.Bacc("TRN2", target_bir_lowering=False, num_devices=1)
    ins, aps = {}, {}
    for name, x in arrays.items():
        x = np.ascontiguousarray(x)
        ins["in_" + name] = x
        aps[name] = nc.dram_tensor("in_" + name, x.shape, mybir.dt.from_np(x.dtype), kind="ExternalInput").ap()
    aps["out"] = nc.dram_tensor("out", _OUT, F32, kind="ExternalOutput").ap()
    build(nc, aps)
    return _run(nc, [ins], core_ids=[0]).results[0]["out"]
```

```python
from contextlib import ExitStack

import numpy as np

import concourse.bass as bass
from concourse import mybir
from concourse.alu_op_type import AluOpType as ALU

F32 = mybir.dt.float32
F16 = mybir.dt.float16
BF16 = mybir.dt.bfloat16
U32 = mybir.dt.uint32
ACT = mybir.ActivationFunctionType
AX = mybir.AxisListType

BATCH, SEQ, C = 4, 256, 512
P = 128
TILES = SEQ // P
CH = C // P
HEADS, HD = 32, 16
KV_HEADS = 8
GROUP = 4
PAIRS = GROUP // 2
GROUPS = HEADS // GROUP
BLK = 64
MAXROW = 3 * HD
VW = 2 * HD + 1
PIECE = 512
EXPERTS = 8
RANK, LORA = 16, 4
LORA_SCALE = 16.0 / RANK ** 0.5
EPS = 1e-5
NEG = -1e30

PRODUCTS = 3 * CH
FIRST, SECOND = 3, 7

XS, WS = 16.0, 128.0
OUT = 1.0 / (XS * WS)

W_QKV0, W_O0, W_EXP, W_QKV1, W_O1 = 1536, 512, EXPERTS * 512, 768, 512
ROUTER_AT = EXPERTS
A_AT = EXPERTS + 4
W_SMALL = A_AT + 64


def build(nc, a):
    ctx = ExitStack()
    with ctx:
        def sb(name, shape, dt=F32):
            return ctx.enter_context(nc.sbuf_tensor(name, shape, dt))

        def ps(name, shape, dt=F32):
            return ctx.enter_context(nc.psum_tensor(name, shape, dt))

        w_qkv0 = sb("w_qkv0", [P, 2, CH, W_QKV0], F16)
        w_o0 = sb("w_o0", [P, 2, CH, W_O0], F16)
        w_exp = sb("w_exp", [P, 2, CH, W_EXP], F16)
        w_qkv1 = sb("w_qkv1", [P, 2, CH, W_QKV1], F16)
        w_o1 = sb("w_o1", [P, 2, CH, W_O1], F16)
        w_small = sb("w_small", [P, 2, CH, W_SMALL], F16)
        w_b = sb("w_b", [P, 2, 512], F16)
        B_EXP, B_O, B_Q, B_KV = 0, 32, 64, 96
        bias = sb("bias", [P, 2, 512], F16)

        ident32 = sb("ident32", [P, P])
        ident16 = sb("ident16", [P, P], F16)
        identb = sb("identb", [P, P], BF16)
        ones = sb("ones", [P, P], F16)
        mask_qk = sb("mask_qk", [P, P], BF16)
        mask_kq = sb("mask_kq", [P, P], BF16)
        rope0 = sb("rope0", [P, TILES, 3])
        cos1 = sb("cos1", [P, TILES, HD])
        sin1 = sb("sin1", [P, TILES, HD])
        gate_bias = sb("gate_bias", [P, EXPERTS])
        iota8 = sb("iota8", [P, 8])
        minus_half = sb("minus_half", [P, TILES])

        rot = sb("rot", [P, 1024])
        rot_t = rot[:].rearrange("p (t c) -> p t c", t=TILES)
        x0 = sb("x0", [P, TILES, C])
        cosx = x0[:].rearrange("p t c -> p (t c)")[:, 0:HD * (HEADS + KV_HEADS)]
        ffn = sb("ffn", [P, TILES, C])
        th = sb("th", [P, C])
        stats = sb("stats", [P, TILES, 6])
        mv = sb("mv", [P, TILES, 2])
        var_eps = sb("var_eps", [P, TILES])
        rstd = sb("rstd", [P, TILES])
        aT = [sb(f"aT{l}", [P, 2, CH, SEQ], F16) for l in range(2)]
        xT = [sb("xT0", [P, 2, CH, SEQ], F16), aT[1]]
        qs = [sb(f"qs{l}", [P, TILES, HEADS, BLK], F16) for l in range(2)]
        ks = [sb("ks0", [P, TILES, HEADS, BLK], F16), sb("ks1", [P, TILES, KV_HEADS, BLK], F16)]
        vs = [sb("vs0", [P, TILES, HEADS, VW], F16), sb("vs1", [P, TILES, KV_HEADS, VW], F16)]
        qT = [sb(f"qT{i}", [P, PAIRS, SEQ], F16) for i in range(2)]
        kT = [sb(f"kT{i}", [P, PAIRS, 2, SEQ], F16) for i in range(2)]
        qmT = sb("qmT", [P, PAIRS, SEQ], F16)
        neg_max = sb("neg_max", [P, TILES, GROUP])
        p32 = sb("p32", [P, 3 * 512])
        p_hi = [sb(f"p_hi{i}", [P, 3 * 512], F16) for i in range(2)]
        p_lo = sb("p_lo", [P, 3 * 512], F16)
        recip = sb("recip", [P, TILES, GROUP])
        o_sum = sb("o_sum", [P, TILES, GROUP, HD])
        attn = [sb(f"attn{l}", [P, TILES, P]) for l in range(2)]
        logits = [sb(f"logits{l}", [P, TILES, 8]) for l in range(2)]
        top = [sb(f"top{l}", [P, TILES, 8]) for l in range(2)]
        top_at = [sb(f"top_at{l}", [P, TILES, 8], U32) for l in range(2)]
        top_f = [sb(f"top_f{l}", [P, TILES, 2]) for l in range(2)]
        chosen = sb("chosen", [P, TILES, EXPERTS])
        chosen16 = sb("chosen16", [P, TILES, EXPERTS], F16)
        chosenT = sb("chosenT", [EXPERTS, SEQ], F16)
        r_bias = sb("r_bias", [P, TILES])
        r_exp = sb("r_exp", [P, TILES, LORA])
        r_sel = sb("r_sel", [P, TILES, LORA])
        r_gate = sb("r_gate", [P, TILES, LORA])
        r_sum = sb("r_sum", [P, TILES])
        r_rec = sb("r_rec", [P, TILES])
        mid16 = sb("mid16", [P, TILES, 2, LORA * RANK], F16)
        midT = sb("midT", [P, SEQ], F16)
        mid = o_sum[:].rearrange("p t h d -> p t (h d)")
        slots = [qs[1][:, t, :, :].rearrange("p h k -> p (h k)").bitcast(F32)[:, PIECE * i:PIECE * (i + 1)]
                 for t in range(TILES) for i in range(2)] + [ks[1][:].rearrange("p t h k -> p (t h k)").bitcast(F32)]

        psB = ps("psB", [P, 3, 512])
        psS = ps("psS", [P, 2, 512])
        psT = ps("psT", [P, 512])
        psO = ps("psO", [P, 512])
        psW = ps("psW", [P, 512])
        tT = psT[:, :].bitcast(F16)
        tO = psO[:, :].bitcast(F16)
        o_ps = psO[:, 0:TILES * GROUP * VW].rearrange("p (t h v) -> p t h v", t=TILES, h=GROUP)
        xn_ps = [[psT[:, :], psW[:, :]], [psW[:, :], psB[:, 0, :]]]
        out_ps = [[psS[:, t, :] for t in range(TILES)], [psB[:, t, :] for t in range(TILES)]]
        delta_ps = [psW[:, :], psT[:, :]]
        small_at = [[(8 * t, 8 * t + EXPERTS) for t in range(TILES)],
                    [((W_SMALL - ROUTER_AT) * t, (W_SMALL - ROUTER_AT) * (t + 1)) for t in range(TILES)]]
        qk_ps = [[psB[:, 0:2, :], psS[:, :, :]], [psB[:, 1:3, :], psS[:, :, :]]]
        qk_ps = [[y.rearrange("p a n -> p (a n)") for y in x] for x in qk_ps]
        v_ps = [[psB[:, 2, :], psT[:, :]], [qk_ps[1][t][:, 640:768] for t in range(TILES)]]

        both = """xn bn mv var rstd xt_ps xt_hi xt_lo proj small rope v_hi v_lo qk_hi qk_lo logits top top_at top_f
            attn at_ps at_hi at_lo out th gated weighed"""
        one = """const x_rot x_in x_st x_out w_hi w_lo made cleared masks rot cosx swap
            chosen chosen_T chosenT ffn_bias ffn_in expert mixed resid
            t1 q_t k_t s_ps s_max max_hi max_lo t2 qm_t st p32 p_hi p_lo pv recip o_lo o_sum
            r_bias r_exp r_first r_sel r_eg r_sum r_rec r_gate mid mid_hi mid_lo mid_ps midT delta"""
        names = one.split() + [n + l for n in both.split() for l in "01"] + [f"staged{i}" for i in range(len(slots))]
        s = {n: ctx.enter_context(nc.semaphore("s_" + n)) for n in names}
        block = ctx.enter_context(nc.Block())

        work, until = [], {}

        def weight(name, dst, src, lo, hi):
            for c in range(CH):
                for at in range(lo, hi, PIECE):
                    to = min(at + PIECE, hi)
                    work.append((dst[:, :, c, at:to], [(src[c * P:(c + 1) * P, at:to], 0, P, 0, to - at)]))
            until[name] = len(work)

        for c in range(CH):
            rows = slice(c * P, (c + 1) * P)
            work.append((w_small[:, :, c, :], [(a["gate"][rows, :], 0, P, 0, EXPERTS), (a["router"][rows, :], 0, P, ROUTER_AT, A_AT),
                                               (a["A"][rows, :], 0, P, A_AT, W_SMALL)]))
        until["small"] = len(work)
        weight("qkv0", w_qkv0, a["wqkv0"], 0, W_QKV0)
        for at, n, name, lo, hi in ((B_EXP, EXPERTS, "expert_b", 0, 512), (B_O, 1, "b_o1", 0, 512), (B_Q, 1, "b_qkv1", 0, 512),
                                    (B_KV, 1, "b_qkv1", 512, 768)):
            work.append((bias[at:at + n, :, 0:hi - lo], [(a[name][:, lo:hi], at, at + n, 0, hi - lo)]))
        until["bias"] = len(work)
        for e in range(EXPERTS):
            weight(f"exp{e}", w_exp, a["wexp"], 512 * e, 512 * (e + 1))
            if e == 1:
                weight("o0", w_o0, a["wo0"], 0, W_O0)
            if e == 3:
                weight("o1", w_o1, a["wo1"], 0, W_O1)
            if e == 5:
                work.append((w_b[:, :, :], [(a["B"], 0, 64, 0, 512), (a["B"], 64, P, 0, 512)]))
        weight("qkv1", w_qkv1, a["wqkv1"], 0, W_QKV1)
        N = len(work)
        landed, landed_by = [0] * len(slots), []
        for i, (_, parts) in enumerate(work):
            landed[i % len(slots)] += 16 * len(parts)
            landed_by.append(landed[i % len(slots)])
        split_by = [until["exp0"]] + [until[f"exp{e}"] for e in range(1, EXPERTS)] + [N]

        def staged(i):
            return s[f"staged{i % len(slots)}"]

        def piece(i):
            dst, parts = work[i]
            return dst, slots[i % len(slots)][parts[0][1]:parts[-1][2], 0:parts[-1][4]]

        def heads(x, lo, hi):
            return x[:, lo:hi].rearrange("p (h d) -> p h d", d=HD)

        def turns(b0, b1):
            layers = [l for l, b in ((0, b0), (1, b1)) if b is not None]
            return [(l, g) for g in range(GROUPS) for l in layers]

        def chunk_after(order, k):
            j = k - 3
            return j if 0 <= j < len(order) and order[j][1] % 2 else None

        def units(order, k):
            n = len(order)
            per = EXPERTS * TILES // n
            return [divmod(u, TILES) for u in range(per * k, per * (k + 1))]

        def rounds(eng, run):
            run(0, None, 0)
            with eng.Fori(1, BATCH - 1) as b:
                run(b, b - 1, 16 * b - 8)
            run(BATCH - 1, BATCH - 2, 16 * BATCH - 24)
            run(None, BATCH - 1, 16 * BATCH - 8)

        def more(b0):
            return not (b0 is None or isinstance(b0, int) and b0 == BATCH - 1)

        def seq(name, b):
            if isinstance(b, int):
                return a[name][b].rearrange("(t p) c -> p t c", p=P)
            return a[name][bass.ds(b, 1)].rearrange("b (t p) c -> p (b t) c", p=P)

        @block.sync
        def _(sp):
            for dst, src in ((ident32, "ident"), (rope0, "rope0"), (cos1, "cos1"), (sin1, "sin1"), (iota8, "iota8")):
                sp.dma_start(dst[:], a[src]).then_inc(s["const"], 16)
            sp.dma_start(gate_bias[:], a["gate_b"].partition_broadcast(P)).then_inc(s["const"], 16)
            sp.dma_start(rot_t, seq("x", 0)).then_inc(s["x_rot"], 16)

            def load(lo, hi):
                for i in range(lo, hi):
                    if i >= len(slots):
                        sp.wait_ge(s["w_lo"], i - len(slots) + 1)
                    for src, p0, p1, c0, c1 in work[i][1]:
                        sp.dma_start(slots[i % len(slots)][p0:p1, c0:c1], src).then_inc(staged(i), 16)

            def run(b0, b1, n0):
                if b0 is not None:
                    if b1 is None:
                        load(0, until["exp2"])
                    else:
                        sp.wait_ge(s["rope1"], 2 * b1 + 2)
                    sp.dma_start(x0[:], seq("x", b0)).then_inc(s["x_in"], 16)
                    if more(b0):
                        sp.wait_ge(s["qk_lo0"], 2 * b0 + 2)
                        if b1 is not None:
                            sp.wait_ge(s["qk_lo1"], 2 * b1 + 2)
                        sp.dma_start(rot_t, seq("x", b0 + 1)).then_inc(s["x_rot"], 16)
                    if b1 is None:
                        load(until["exp2"], N)
                    sp.wait_ge(s["resid"], 2 * b0 + 2)
                    sp.dma_start(seq("out", b0), x0[:]).then_inc(s["x_st"], 16)

            rounds(sp, run)

        @block.gpsimd
        def _(pool):
            pool.memset(mask_qk[:], 0.0).then_inc(s["masks"], 1)
            pool.memset(mask_kq[:], 0.0).then_inc(s["masks"], 1)
            pool.memset(minus_half[:], -0.5).then_inc(s["masks"], 1)
            pool.wait_ge(s["masks"], 3)
            pool.affine_select(out=mask_qk[:], in_=mask_qk[:], compare_op=ALU.is_ge, fill=NEG, base=0,
                               pattern=[[-1, P]], channel_multiplier=1).then_inc(s["masks"], 1)
            pool.affine_select(out=mask_kq[:], in_=mask_kq[:], compare_op=ALU.is_ge, fill=NEG, base=0,
                               pattern=[[1, P]], channel_multiplier=-1).then_inc(s["masks"], 1)

            def clear(l):
                for t in range(TILES):
                    pool.memset(ks[l][:, t, :, MAXROW:MAXROW + 2], 1.0)
                    pool.memset(ks[l][:, t, :, MAXROW + 2:BLK], 0.0)
                    last = pool.memset(qs[l][:, t, :, MAXROW + 2:BLK], 0.0)
                last.then_inc(s["cleared"], 1)

            clear(0)

            def rms(l, m):
                pool.wait_ge(s[f"var{l}"], m + 1)
                pool.tensor_tensor(rstd[:], var_eps[:], minus_half[:], ALU.pow).then_inc(s[f"rstd{l}"], 1)

            def split_qk(l, b, t):
                pool.wait_ge(s[f"qk_hi{l}"], 2 * b + t + 1)
                pool.tensor_tensor(qs[l][:, t, :, HD:2 * HD], heads(rot, 0, 512), qs[l][:, t, :, 0:HD], ALU.subtract)
                pool.tensor_tensor(ks[l][:, t, :, 2 * HD:3 * HD], heads(rot, 512, 1024 if l == 0 else 640), ks[l][:, t, :, 0:HD],
                                   ALU.subtract).then_inc(s[f"qk_lo{l}"], 1)

            rms(0, 0)

            def run(b0, b1, n0):
                order = turns(b0, b1)
                for l, b in ((0, b0), (1, b1)):
                    if b is not None:
                        for t in range(TILES):
                            split_qk(l, b, t)
                            pool.memset(qs[l][:, t, :, MAXROW:MAXROW + 2], 0.0).then_inc(s["cleared"], 1)
                for k in range(len(order)):
                    n = n0 + k
                    pool.wait_ge(s["p32"], n + 1)
                    pool.wait_ge(s["pv"], n)
                    pool.tensor_tensor(p_lo[:], p32[:], p_hi[k % 2][:], ALU.subtract).then_inc(s["p_lo"], 1)
                    if more(b0) and k == len(order) // 2 + 1:
                        rms(0, b0 + 1)
                if b1 is None:
                    pool.wait_ge(s["w_lo"], N)
                    clear(1)
                if b0 is not None:
                    rms(1, b0)
                if b1 is not None:
                    pool.wait_ge(s["x_st"], 16 * b1 + 16)
                    pool.wait_ge(s["weighed1"], 2 * b1 + 2)
                    pool.dma_start(seq("out", b1), p32[:, 0:TILES * C].rearrange("p (t c) -> p t c", t=TILES),
                                   accum_op=ALU.add).then_inc(s["x_out"], 16)

            rounds(pool, run)
            pool.wait_ge(s["x_out"], BATCH * 16)
            pool.wait_ge(s["x_st"], BATCH * 16)

        @block.scalar
        def _(act):
            def split(lo, hi):
                for i in range(lo, hi):
                    act.wait_ge(staged(i), landed_by[i])
                    dst, src = piece(i)
                    act.activation(dst[:, 0, :], src, ACT.Copy, scale=WS).then_inc(s["w_hi"], 1)

            def turned(l, b):
                for t in range(TILES):
                    act.wait_ge(s[f"xt_ps{l}"], 2 * b + t + 1)
                    act.activation(xT[l][:, 0, :, t * P:(t + 1) * P], xn_ps[l][t].rearrange("p (c n) -> p c n", c=CH),
                                   ACT.Copy, scale=XS).then_inc(s[f"xt_hi{l}"], 1)

            def heads_hi(l, b, t):
                act.wait_ge(s[f"proj{l}"], 2 * b + t + 1)
                act.activation(vs[l][:, t, :, 0:HD], heads(v_ps[l][t], 0, 512 if l == 0 else 128), ACT.Copy,
                               scale=OUT).then_inc(s[f"v_hi{l}"], 1)
                act.wait_ge(s[f"rope{l}"], 2 * b + t + 1)
                for j in range(2):
                    act.activation(ks[l][:, t, :, j * HD:(j + 1) * HD], heads(rot, 512, 1024 if l == 0 else 640), ACT.Copy)
                for j in (2, 0):
                    last = act.activation(qs[l][:, t, :, j * HD:(j + 1) * HD], heads(rot, 0, 512), ACT.Copy)
                last.then_inc(s[f"qk_hi{l}"], 1)

            def q_turned(n):
                act.wait_ge(s["t1"], n + 1)
                return tT[:, 0:PAIRS * SEQ].rearrange("p (j n) -> p j n", j=PAIRS)

            def softmax(order, k, n, part):
                scale = HD ** -0.5 if order[k][0] == 0 else 1.0 / HD
                src = psB[:].rearrange("p a n -> p (a n)")
                if part == 0:
                    act.wait_ge(s["st"], n + 1)
                    if n_early(n) is not None:
                        act.wait_ge(s["pv"], n - 1)
                    act.activation(p_hi[k % 2][:], src, ACT.Exp, scale=scale).then_inc(s["p_hi"], 1)
                else:
                    act.wait_ge(s["p_lo"], n)
                    act.activation(p32[:], src, ACT.Exp, scale=scale).then_inc(s["p32"], 1)

            def chunk_hi(order, j, b, g):
                l = order[j][0]
                c = g // 2
                act.wait_ge(s[f"at_ps{l}"], 4 * b + c + 1)
                act.activation(aT[l][:, 0, c, :], psT[:, SEQ:2 * SEQ], ACT.Copy, scale=XS).then_inc(s[f"at_hi{l}"], 1)

            split(0, until["qkv0"])
            act.wait_ge(s["const"], 6 * 16)
            act.wait_ge(s["cleared"], 1)

            def run(b0, b1, n0):
                order = turns(b0, b1)
                bs = (b0, b1)
                if b0 is not None:
                    turned(0, b0)
                    for t in range(TILES):
                        act.wait_ge(s["proj0"], 2 * b0 + t + 1)
                        if t:
                            act.wait_ge(s["qk_lo0"], 2 * b0 + 1)
                        src = qk_ps[0][t].rearrange("p (n two) -> p n two", two=2)
                        dst = rot[:].rearrange("p (n two) -> p n two", two=2)
                        act.activation(dst[:, :, 0], src[:, :, 1], ACT.Copy, scale=rope0[:, t, 1:2])
                        act.activation(dst[:, :, 1], src[:, :, 0], ACT.Copy, scale=rope0[:, t, 2:3]).then_inc(s["rot"], 1)
                        heads_hi(0, b0, t)
                if b1 is not None:
                    turned(1, b1)
                if b0 is not None:
                    act.wait_ge(s["chosen_T"], b0 + 1)
                    act.activation(chosenT[:], tO[0:EXPERTS, 0:SEQ], ACT.Copy, scale=XS).then_inc(s["chosenT"], 1)
                    if b1 is None:
                        split(until["qkv0"], split_by[0])
                    for t in range(TILES):
                        act.wait_ge(s["ffn_bias"], 2 * b0 + t + 1)
                        act.activation(ffn[:, t, :], psW[:], ACT.Copy).then_inc(s["ffn_in"], 1)
                if b1 is not None:
                    act.wait_ge(s["r_bias"], b1 + 1)
                    for t in range(TILES):
                        last = act.activation(r_exp[:, t, :], logits[1][:, t, 0:LORA], ACT.Exp, bias=r_bias[:, t:t + 1])
                    last.then_inc(s["r_exp"], 1)
                    for t in range(TILES):
                        heads_hi(1, b1, t)
                    act.wait_ge(s["x_out"], 16 * b1)
                act.activation(qT[0][:], q_turned(n0), ACT.Copy).then_inc(s["q_t"], 1)
                for k in range(len(order) + 3):
                    n = n0 + k
                    if 1 <= k <= len(order):
                        softmax(order, k - 1, n - 1, 0)
                    if k + 1 < len(order):
                        act.activation(qT[(k + 1) % 2][:], q_turned(n + 1), ACT.Copy).then_inc(s["q_t"], 1)
                    if 1 <= k <= len(order):
                        softmax(order, k - 1, n - 1, 1)
                    if k < len(order):
                        act.wait_ge(s["t2"], n + 1)
                        act.activation(qmT[:], tT[:, 0:PAIRS * SEQ].rearrange("p (j n) -> p j n", j=PAIRS), ACT.Copy).then_inc(s["qm_t"], 1)
                    j = chunk_after(order, k)
                    if j is not None:
                        chunk_hi(order, j, bs[order[j][0]], order[j][1])
                    if b1 is None and k < GROUPS:
                        split(split_by[k], split_by[k + 1])
                if b0 is not None:
                    act.wait_ge(s["mixed"], b0 * 16 + 16)
                    for t in range(TILES):
                        if t:
                            act.wait_ge(s["gated0"], 2 * b0 + 1)
                        act.activation(th[:], ffn[:, t, :], ACT.Tanh, scale=0.5 * OUT).then_inc(s["th0"], 1)
                if b1 is not None:
                    act.wait_ge(s["mid_ps"], b1 + 1)
                    act.activation(midT[:], tT[:, 0:SEQ], ACT.Copy).then_inc(s["midT"], 1)
                    for t in range(TILES):
                        act.wait_ge(s["delta"], 2 * b1 + t + 1)
                        if t:
                            act.wait_ge(s["weighed1"], 2 * b1 + 1)
                        elif b0 is not None:
                            act.wait_ge(s["gated0"], 2 * b0 + 2)
                        act.activation(th[:], delta_ps[t], ACT.Tanh, scale=0.5 * OUT).then_inc(s["th1"], 1)

            def n_early(n):
                return None if isinstance(n, int) and n < 2 else n

            rounds(act, run)

        @block.vector
        def _(dve):
            def wait_alone(name, value):
                if not isinstance(value, int):
                    value = dve.snap(value)
                dve.wait_ge(s["const"], 6 * 16)
                dve.wait_ge(s[name], value)

            def split(lo, hi):
                for i in range(lo, hi):
                    dst, src = piece(i)
                    dve.wait_ge(s["w_hi"], i + 1)
                    dve.scalar_tensor_tensor(out=dst[:, 1, :], in0=src, scalar=WS, in1=dst[:, 0, :],
                                             op0=ALU.mult, op1=ALU.subtract).then_inc(s["w_lo"], 1)

            def norm_stats(l, b, t):
                dve.bn_stats(stats[:, t, :], (rot_t, x0)[l][:, t, :]).then_inc(s[f"bn{l}"], 1)

            def norm_var(l, b):
                dve.wait_ge(s[f"bn{l}"], 2 * b + 2)
                dve.memset(var_eps[:], EPS)
                for t in range(TILES):
                    dve.bn_aggr(mv[:, t, :], stats[:, t, :]).then_inc(s[f"mv{l}"], 1)
                dve.wait_ge(s[f"mv{l}"], 2 * b + 2)
                dve.tensor_tensor(var_eps[:], mv[:, :, 1], var_eps[:], ALU.add).then_inc(s[f"var{l}"], 1)

            def norm_x(l, b, t):
                dve.wait_ge(s[f"rstd{l}"], b + 1)
                dve.tensor_scalar((rot_t, ffn)[l][:, t, :], (rot_t, x0)[l][:, t, :], mv[:, t, 0:1], rstd[:, t:t + 1],
                                  ALU.subtract, ALU.mult).then_inc(s[f"xn{l}"], 1)

            def turned(l, b):
                for t in range(TILES):
                    at = slice(t * P, (t + 1) * P)
                    dve.wait_ge(s[f"xt_hi{l}"], 2 * b + t + 1)
                    dve.scalar_tensor_tensor(out=xT[l][:, 1, :, at], in0=xn_ps[l][t].rearrange("p (c n) -> p c n", c=CH),
                                             scalar=XS, in1=xT[l][:, 0, :, at], op0=ALU.mult, op1=ALU.subtract).then_inc(s[f"xt_lo{l}"], 1)

            def v_low(l, b, t):
                dve.wait_ge(s[f"v_hi{l}"], 2 * b + t + 1)
                dve.scalar_tensor_tensor(out=vs[l][:, t, :, HD + 1:VW], in0=heads(v_ps[l][t], 0, 512 if l == 0 else 128),
                                         scalar=OUT, in1=vs[l][:, t, :, 0:HD], op0=ALU.mult, op1=ALU.subtract).then_inc(s[f"v_lo{l}"], 1)

            def largest(l, b):
                wait_alone(f"logits{l}", 2 * b + 2)
                for t in range(TILES):
                    dve.max(top[l][:, t, :], logits[l][:, t, :]).then_inc(s[f"top{l}"], 1)
                wait_alone(f"top{l}", 2 * b + 2)
                for t in range(TILES):
                    dve.max_index(top_at[l][:, t, :], top[l][:, t, :], logits[l][:, t, :]).then_inc(s[f"top_at{l}"], 1)
                dve.wait_ge(s[f"top_at{l}"], 2 * b + 2)
                dve.tensor_copy(top_f[l][:], top_at[l][:, :, 0:2]).then_inc(s[f"top_f{l}"], 1)

            def choose(b):
                dve.wait_ge(s["small0"], b + 1)
                for t in range(TILES):
                    lo, hi = small_at[0][t]
                    dve.scalar_tensor_tensor(out=logits[0][:, t, :], in0=psO[:, lo:hi], scalar=OUT,
                                             in1=gate_bias[:], op0=ALU.mult, op1=ALU.add).then_inc(s["logits0"], 1)
                largest(0, b)
                dve.wait_ge(s["top_f0"], b + 1)
                for t in range(TILES):
                    dve.tensor_scalar(chosen[:, t, :], iota8[:], top_f[0][:, t, 0:1], None, ALU.is_equal)
                    last = dve.tensor_scalar(chosen16[:, t, :], iota8[:], top_f[0][:, t, 0:1], None, ALU.is_equal)
                last.then_inc(s["chosen"], 1)

            def route(b):
                dve.wait_ge(s["small1"], b + 1)
                for t in range(TILES):
                    lo = small_at[1][t][0]
                    dve.tensor_scalar(logits[1][:, t, 0:LORA], psO[:, lo:lo + LORA], OUT, None, ALU.mult).then_inc(s["logits1"], 1)
                largest(1, b)
                dve.tensor_scalar(r_bias[:], top[1][:, :, 0], -1.0, None, ALU.mult).then_inc(s["r_bias"], 1)
                dve.wait_ge(s["top_f1"], b + 1)
                for t in range(TILES):
                    dve.tensor_scalar(r_sel[:, t, :], iota8[:, 0:LORA], top_f[1][:, t, 0:1], None, ALU.is_equal).then_inc(s["r_first"], 1)
                dve.wait_ge(s["r_first"], 2 * b + 2)
                for t in range(TILES):
                    dve.scalar_tensor_tensor(out=r_sel[:, t, :], in0=iota8[:, 0:LORA], scalar=top_f[1][:, t, 1:2], in1=r_sel[:, t, :],
                                             op0=ALU.is_equal, op1=ALU.add).then_inc(s["r_sel"], 1)
                dve.wait_ge(s["r_sel"], 2 * b + 2)
                dve.wait_ge(s["r_exp"], b + 1)
                dve.tensor_tensor(r_exp[:], r_exp[:], r_sel[:], ALU.mult).then_inc(s["r_eg"], 1)
                dve.wait_ge(s["r_eg"], b + 1)
                dve.tensor_reduce(r_sum[:], r_exp[:], AX.X, ALU.add).then_inc(s["r_sum"], 1)
                dve.wait_ge(s["r_sum"], b + 1)
                dve.reciprocal(r_rec[:], r_sum[:]).then_inc(s["r_rec"], 1)
                dve.wait_ge(s["r_rec"], b + 1)
                for t in range(TILES):
                    dve.tensor_scalar(r_gate[:, t, :], r_exp[:, t, :], r_rec[:, t:t + 1], LORA_SCALE * OUT * XS,
                                      ALU.mult, ALU.mult).then_inc(s["r_gate"], 1)
                dve.wait_ge(s["r_gate"], 2 * b + 2)
                for t in range(TILES):
                    lo, hi = small_at[1][t]
                    dve.tensor_tensor(mid[:, t, :].rearrange("p (e r) -> p e r", e=LORA),
                                      psO[:, lo + LORA:hi].rearrange("p (e r) -> p e r", e=LORA),
                                      r_gate[:, t, :].unsqueeze(2).broadcast_to([P, LORA, RANK]), ALU.mult).then_inc(s["mid"], 1)
                dve.wait_ge(s["mid"], 2 * b + 2)
                dve.tensor_copy(mid16[:, :, 0, :], mid[:]).then_inc(s["mid_hi"], 1)
                dve.wait_ge(s["mid_hi"], b + 1)
                dve.tensor_tensor(mid16[:, :, 1, :], mid[:], mid16[:, :, 0, :], ALU.subtract).then_inc(s["mid_lo"], 1)

            def rotate1(b, t):
                n_h, half = HEADS + KV_HEADS, HD // 2
                dve.wait_ge(s["v_hi1"], 2 * b + t + 1)
                src, dst = heads(qk_ps[1][t], 0, HD * n_h), heads(rot, 0, HD * n_h)
                for lo in (0, half):
                    hi = half - lo
                    last = dve.tensor_tensor(dst[:, :, lo:lo + half], src[:, :, hi:hi + half],
                                             sin1[:, t, lo:lo + half].unsqueeze(1).broadcast_to([P, n_h, half]), ALU.mult)
                last.then_inc(s["swap"], 1)
                dve.tensor_tensor(heads(cosx, 0, HD * n_h), src,
                                  cos1[:, t, :].unsqueeze(1).broadcast_to([P, n_h, HD]), ALU.mult).then_inc(s["cosx"], 1)
                dve.wait_ge(s["cosx"], 2 * b + t + 1)
                dve.tensor_tensor(rot[:, 0:HD * n_h], cosx, rot[:, 0:HD * n_h], ALU.add).then_inc(s["rope1"], 1)

            def k_turned(order, k, n):
                dve.wait_ge(s["q_t"], n + 1)
                w = PAIRS if order[k][0] == 0 else 1
                src = tT[:, PAIRS * SEQ:(PAIRS + w) * SEQ].rearrange("p (j n) -> p j n", j=w)
                dve.tensor_copy(kT[k % 2][0:64, 0:w, 0, :], src[0:64])
                dve.tensor_copy(kT[k % 2][64:P, 0:w, 1, :], src[64:P]).then_inc(s["k_t"], 1)

            def maxima(order, k, n):
                for j in range(3):
                    dve.wait_ge(s["s_ps"], 3 * n + j + 1)
                    if j == 0:
                        out, src = neg_max[:, 0, :], psS[:, k % 2, :].rearrange("p (h k) -> p h k", h=GROUP)
                    else:
                        out = neg_max[:, 1, PAIRS * (j - 1):PAIRS * j]
                        src = psS[:, (k + j) % 2, :].rearrange("p (h k) -> p h k", h=PAIRS)
                    dve.tensor_reduce(out, src, AX.X, ALU.max, negate=True).then_inc(s["s_max"], 1)

            def max_rows(order, k, n):
                l, g = order[k]
                at = slice(GROUP * g, GROUP * (g + 1))
                dve.wait_ge(s["s_max"], 3 * n + 3)
                dve.tensor_copy(qs[l][:, :, at, MAXROW], neg_max[:]).then_inc(s["max_hi"], 1)
                dve.wait_ge(s["max_hi"], n + 1)
                dve.tensor_tensor(qs[l][:, :, at, MAXROW + 1], neg_max[:], qs[l][:, :, at, MAXROW], ALU.subtract).then_inc(s["max_lo"], 1)

            def outputs(order, k, n, b):
                l, g = order[k]
                dve.wait_ge(s["pv"], n + 1)
                dve.tensor_copy(o_sum[:], o_ps[:, :, :, HD + 1:VW]).then_inc(s["o_lo"], 1)
                dve.reciprocal(recip[:], o_ps[:, :, :, HD]).then_inc(s["recip"], 1)
                dve.wait_ge(s["o_lo"], n + 1)
                dve.tensor_tensor(o_sum[:], o_ps[:, :, :, 0:HD], o_sum[:], ALU.add).then_inc(s["o_sum"], 1)
                dve.wait_ge(s["o_sum"], n + 1)
                dve.wait_ge(s["recip"], n + 1)
                if g % 2 == 0:
                    dve.wait_ge(s[f"at_ps{l}"], 4 * b + g // 2)
                at = GROUP * HD * (g % 2)
                dst = attn[l][:, :, at:at + GROUP * HD].rearrange("p t (h d) -> p t h d", d=HD)
                dve.tensor_tensor(dst, o_sum[:], recip[:].unsqueeze(3).broadcast_to([P, TILES, GROUP, HD]), ALU.mult).then_inc(s[f"attn{l}"], 1)

            def chunk_lo(order, j, b):
                l, g = order[j]
                c = g // 2
                dve.wait_ge(s[f"at_hi{l}"], 4 * b + c + 1)
                dve.scalar_tensor_tensor(out=aT[l][:, 1, c, :], in0=psT[:, SEQ:2 * SEQ], scalar=XS, in1=aT[l][:, 0, c, :],
                                         op0=ALU.mult, op1=ALU.subtract).then_inc(s[f"at_lo{l}"], 1)

            def mix(b, e, t):
                m = 16 * b + (2 * e + t)
                dve.wait_ge(s["expert"], m + 1)
                if e:
                    dve.wait_ge(s["mixed"], m - 1)
                dve.scalar_tensor_tensor(out=ffn[:, t, :], in0=psW[:], scalar=chosen[:, t, e:e + 1], in1=ffn[:, t, :],
                                         op0=ALU.mult, op1=ALU.add).then_inc(s["mixed"], 1)

            def constants():
                for i in range(2):
                    dve.memset(kT[i][64:P, :, 0, :], 0.0)
                    dve.memset(kT[i][0:64, :, 1, :], 0.0)
                for l in range(2):
                    dve.memset(vs[l][:, :, :, HD:HD + 1], 1.0)
                dve.memset(logits[1][:, :, LORA:8], NEG)
                dve.memset(ones[:], XS)
                dve.memset(w_b[64:P, 1, :], 0.0)
                dve.wait_ge(s["const"], 6 * 16)
                dve.tensor_copy(ident16[:], ident32[:])
                dve.tensor_copy(identb[:], ident32[:]).then_inc(s["made"], 1)

            constants()
            dve.wait_ge(s["x_rot"], 16)
            for t in range(TILES):
                norm_stats(0, 0, t)
            norm_var(0, 0)
            for t in range(TILES):
                norm_x(0, 0, t)
            split(0, until["qkv0"])

            def run(b0, b1, n0):
                order = turns(b0, b1)
                bs = (b0, b1)
                size = len(order)
                if b0 is not None:
                    turned(0, b0)
                    choose(b0)
                    for t in range(TILES):
                        dve.wait_ge(s["rot"], 2 * b0 + t + 1)
                        dve.scalar_tensor_tensor(out=rot[:], in0=qk_ps[0][t], scalar=rope0[:, t, 0:1],
                                                 in1=rot[:], op0=ALU.mult, op1=ALU.add).then_inc(s["rope0"], 1)
                        v_low(0, b0, t)
                if b1 is None:
                    split(until["qkv0"], split_by[0])
                if b1 is not None:
                    turned(1, b1)
                    route(b1)
                    dve.wait_ge(s["x_st"], 16 * b1 + 16)
                    for t in range(TILES):
                        if t:
                            dve.wait_ge(s["qk_lo1"], 2 * b1 + 1)
                        elif b0 is not None:
                            dve.wait_ge(s["qk_lo0"], 2 * b0 + 2)
                        rotate1(b1, t)
                        v_low(1, b1, t)
                k_turned(order, 0, n0)
                for k in range(size + 3):
                    n = n0 + k
                    if k < size:
                        maxima(order, k, n)
                        if k + 1 < size:
                            k_turned(order, k + 1, n + 1)
                        max_rows(order, k, n)
                    late = size == GROUPS
                    if not late and 2 <= k < size + 2:
                        outputs(order, k - 2, n - 2, bs[order[k - 2][0]])
                    if b0 is not None and k < size:
                        for e, t in units(order, k):
                            mix(b0, e, t)
                    if late and 2 <= k < size + 2:
                        outputs(order, k - 2, n - 2, bs[order[k - 2][0]])
                    j = chunk_after(order, k)
                    if j is not None:
                        chunk_lo(order, j, bs[order[j][0]])
                    if b1 is None and k < GROUPS:
                        split(split_by[k], split_by[k + 1])
                    if more(b0):
                        half = size // 2
                        if k == half - 2:
                            dve.wait_ge(s["x_rot"], 16 * b0 + 32)
                            norm_stats(0, b0 + 1, 0)
                        if k == half - 1:
                            norm_stats(0, b0 + 1, 1)
                        if k == half:
                            norm_var(0, b0 + 1)
                        if k == half + 2:
                            norm_x(0, b0 + 1, 0)
                        if k == half + 3:
                            norm_x(0, b0 + 1, 1)
                if b0 is not None:
                    for t in range(TILES):
                        m = 2 * b0 + t
                        dve.wait_ge(s["th0"], m + 1)
                        dve.scalar_tensor_tensor(out=ffn[:, t, :], in0=th[:], scalar=1.0, in1=ffn[:, t, :],
                                                 op0=ALU.add, op1=ALU.mult).then_inc(s["gated0"], 1)
                    for t in range(TILES):
                        m = 2 * b0 + t
                        dve.wait_ge(s["gated0"], m + 1)
                        dve.wait_ge(s["out0"], m + 1)
                        dve.scalar_tensor_tensor(out=ffn[:, t, :], in0=out_ps[0][t], scalar=0.5 * OUT * OUT, in1=ffn[:, t, :],
                                                 op0=ALU.mult, op1=ALU.mult).then_inc(s["weighed0"], 1)
                        dve.wait_ge(s["weighed0"], m + 1)
                        dve.wait_ge(s["x_in"], 16 * b0 + 16)
                        dve.tensor_tensor(x0[:, t, :], x0[:, t, :], ffn[:, t, :], ALU.add).then_inc(s["resid"], 1)
                        dve.wait_ge(s["resid"], m + 1)
                        norm_stats(1, b0, t)
                    norm_var(1, b0)
                    for t in range(TILES):
                        norm_x(1, b0, t)
                if b1 is not None:
                    for t in range(TILES):
                        m = 2 * b1 + t
                        dve.wait_ge(s["th1"], m + 1)
                        dve.scalar_tensor_tensor(out=th[:], in0=th[:], scalar=1.0, in1=delta_ps[t],
                                                 op0=ALU.add, op1=ALU.mult).then_inc(s["gated1"], 1)
                        dve.wait_ge(s["gated1"], m + 1)
                        dve.wait_ge(s["out1"], m + 1)
                        dve.scalar_tensor_tensor(out=p32[:, C * t:C * (t + 1)], in0=out_ps[1][t], scalar=0.5 * OUT * OUT, in1=th[:],
                                                 op0=ALU.mult, op1=ALU.mult).then_inc(s["weighed1"], 1)

            rounds(dve, run)

        @block.tensor
        def _(pe):
            pe.wait_ge(s["made"], 1)
            pe.wait_ge(s["masks"], 5)

            def product(outs, lhs, t, rhs, start=True, part=(0, PRODUCTS)):
                at = slice(t * P, (t + 1) * P)
                steps = [(c, i, j) for c in range(CH) for i, j in ((0, 0), (0, 1), (1, 0))]
                for c, i, j in steps[slice(*part)]:
                    for out, (w, lo, hi) in zip(outs, rhs):
                        last = pe.matmul(out, lhs[:, i, c, at], w[:, j, c, lo:hi], start=start and (c, i, j) == steps[0],
                                         stop=(c, i, j) == steps[-1])
                return last

            def add_row(out, row):
                for j in range(2):
                    pe.matmul(out, ones[row:row + 1, :], bias[row:row + 1, j, 0:out.shape[1]], start=j == 0, stop=False)

            def turn_x(l, b, t):
                src = (rot_t, ffn)[l]
                pe.wait_ge(s[f"xn{l}"], 2 * b + t + 1)
                for c in range(CH):
                    last = pe.transpose(xn_ps[l][t][:, c * P:(c + 1) * P], src[:, t, c * P:(c + 1) * P], ident32[:])
                last.then_inc(s[f"xt_ps{l}"], 1)

            def turn_q(l, g):
                for j in range(PAIRS):
                    for t in range(TILES):
                        h = GROUP * g + 2 * j
                        last = pe.transpose(tT[:, j * SEQ + t * P:j * SEQ + (t + 1) * P],
                                            qs[l][:, t, h:h + 2, :].rearrange("p h k -> p (h k)"), ident16[:])
                return last

            def turn_qk(order, k, n):
                l, g = order[k]
                pe.wait_ge(s["qm_t"], n - 1 if k else n)
                turn_q(l, g)
                for t in range(TILES):
                    at = PAIRS * SEQ + t * P
                    if l == 0:
                        for j in range(PAIRS):
                            h = GROUP * g + 2 * j
                            last = pe.transpose(tT[:, at + j * SEQ:at + j * SEQ + P],
                                                ks[0][:, t, h:h + 2, :].rearrange("p h k -> p (h k)"), ident16[:])
                    else:
                        for r in range(2):
                            last = pe.transpose(tT[BLK * r:BLK * (r + 1), at:at + P], ks[1][:, t, g, :], ident16[:])
                last.then_inc(s["t1"], 1)

            def scores(order, k, n, between):
                l = order[k][0]
                q, kk = qT[k % 2], kT[k % 2]
                pe.wait_ge(s["k_t"], n + 1)
                pe.wait_ge(s["s_max"], 3 * n - 1) if k else None
                bank = psS[:, k % 2, :]
                pe.matmul(bank.rearrange("p (h k) -> p h k", h=GROUP), identb[:], mask_qk[:].unsqueeze(1).broadcast_to([P, GROUP, P]),
                          start=True, stop=False, skip_group_check=True)
                for j in range(PAIRS):
                    last = pe.matmul(bank[:, 2 * P * j:2 * P * (j + 1)].rearrange("p (h k) -> p h k", h=2), q[:, j, 0:P],
                                     kk[:, j if l == 0 else 0, :, 0:P], start=False, stop=True, skip_group_check=True)
                last.then_inc(s["s_ps"], 1)
                for j in range(PAIRS):
                    if j:
                        between()
                    if j or k:
                        pe.wait_ge(s["s_max"], 3 * n + j)
                    bank = psS[:, (k + 1 + j) % 2, :].rearrange("p (h k) -> p h k", h=2)
                    pe.matmul(bank[:, :, P:SEQ], identb[:], mask_qk[:].unsqueeze(1).broadcast_to([P, 2, P]), start=True, stop=False,
                              skip_group_check=True)
                    pe.matmul(bank, q[:, j, P:SEQ], kk[:, j if l == 0 else 0, :, :], start=False, stop=True,
                              skip_group_check=True).then_inc(s["s_ps"], 1)

            def scores_t(order, k, n):
                l = order[k][0]
                kk = kT[k % 2]
                pe.wait_ge(s["qm_t"], n + 1)
                pe.wait_ge(s["p32"], n)
                for j in range(PAIRS):
                    out = psB[:, j, :].rearrange("p (h q) -> p h q", h=2)
                    pe.matmul(out[:, :, 0:P], identb[:], mask_kq[:].unsqueeze(1).broadcast_to([P, 2, P]), start=True, stop=False,
                              skip_group_check=True)
                    for h in range(2):
                        pe.matmul(out[:, h, :], kk[:, j if l == 0 else 0, h, 0:P], qmT[:, j, :], start=False, stop=True,
                                  skip_group_check=True)
                pe.matmul(psB[:, 2, :].rearrange("p (h q) -> p h q", h=GROUP), identb[:],
                          mask_kq[:].unsqueeze(1).broadcast_to([P, GROUP, P]), start=True, stop=False, skip_group_check=True)
                for j in range(PAIRS):
                    for h in range(2):
                        last = pe.matmul(psB[:, 2, P * (2 * j + h):P * (2 * j + h + 1)], kk[:, j if l == 0 else 0, h, P:SEQ],
                                         qmT[:, j, P:SEQ], start=False, stop=True, skip_group_check=True)
                last.then_inc(s["st"], 1)

            def values(order, k, n, b, before):
                l, g = order[k]
                pe.wait_ge(s["p_lo"], n + 1)
                if before is not None:
                    pe.wait_ge(*before)
                for h in range(GROUP):
                    v = GROUP * g + h if l == 0 else g
                    for t in range(TILES):
                        for kt in range(t + 1):
                            at = SEQ * h + P * t if kt == 0 else GROUP * SEQ + P * h
                            pe.matmul(o_ps[:, t, h, :], p_hi[k % 2][:, at:at + P], vs[l][:, kt, v, :], start=kt == 0, stop=False,
                                      skip_group_check=True)
                            last = pe.matmul(o_ps[:, t, h, 0:HD + 1], p_lo[:, at:at + P], vs[l][:, kt, v, 0:HD + 1], start=False,
                                             stop=kt == t, skip_group_check=True)
                last.then_inc(s["pv"], 1)

            def turn_chunk(order, j, b):
                l, g = order[j]
                pe.wait_ge(s[f"attn{l}"], GROUPS * b + g + 1)
                for t in range(TILES):
                    last = pe.transpose(psT[:, SEQ + t * P:SEQ + (t + 1) * P], attn[l][:, t, :], ident32[:])
                last.then_inc(s[f"at_ps{l}"], 1)

            def expert(b, e, t, first, lo=0, hi=PRODUCTS):
                if lo == 0:
                    if first:
                        pe.wait_ge(s["w_lo"], until[f"exp{e}"])
                    pe.wait_ge(s["mixed"], 16 * b + (2 * e + t))
                last = product([psW[:]], xT[0], t, [(w_exp, 512 * e, 512 * (e + 1))], part=(lo, hi))
                if hi == PRODUCTS:
                    last.then_inc(s["expert"], 1)

            def run(b0, b1, n0):
                order = turns(b0, b1)
                bs = (b0, b1)
                size = len(order)
                if b1 is not None:
                    pe.wait_ge(s["weighed1"], 2 * b1)
                if b0 is not None:
                    pe.wait_ge(s["weighed0"], 2 * b0)
                    for t in range(TILES):
                        turn_x(0, b0, t)
                    if b1 is None:
                        pe.wait_ge(s["w_lo"], until["small"])
                    for t in range(TILES):
                        pe.wait_ge(s["xt_lo0"], 2 * b0 + t + 1)
                        last = product([psO[:, slice(*small_at[0][t])]], xT[0], t, [(w_small, 0, EXPERTS)])
                    last.then_inc(s["small0"], 1)
                    if b1 is None:
                        pe.wait_ge(s["w_lo"], until["qkv0"])
                    for t in range(TILES):
                        product([qk_ps[0][t][:, 0:512], qk_ps[0][t][:, 512:1024], v_ps[0][t]], xT[0], t,
                                [(w_qkv0, 512 * i, 512 * (i + 1)) for i in range(3)]).then_inc(s["proj0"], 1)
                if b1 is not None:
                    for t in range(TILES):
                        if b0 is not None and t:
                            pe.wait_ge(s["rope0"], 2 * b0 + 1)
                        turn_x(1, b1, t)
                if b0 is not None:
                    pe.wait_ge(s["chosen"], b0 + 1)
                    for t in range(TILES):
                        last = pe.transpose(tO[0:EXPERTS, t * P:(t + 1) * P], chosen16[:, t, :], ident16[:])
                    last.then_inc(s["chosen_T"], 1)
                    if b1 is None:
                        pe.wait_ge(s["w_lo"], until["bias"])
                    else:
                        pe.wait_ge(s["xt_lo1"], 2 * b1 + 1)
                    pe.wait_ge(s["chosenT"], b0 + 1)
                    for t in range(TILES):
                        pe.wait_ge(s["ffn_in"], 2 * b0 + t)
                        for j in range(2):
                            last = pe.matmul(psW[:], chosenT[:, t * P:(t + 1) * P], bias[0:EXPERTS, j, :], start=j == 0, stop=j == 1)
                        last.then_inc(s["ffn_bias"], 1)
                if b1 is not None:
                    for t in range(TILES):
                        pe.wait_ge(s["xt_lo1"], 2 * b1 + t + 1)
                        last = product([psO[:, slice(*small_at[1][t])]], xT[1], t, [(w_small, ROUTER_AT, W_SMALL)])
                    last.then_inc(s["small1"], 1)
                    for t in range(TILES):
                        if b0 is not None:
                            pe.wait_ge(s["rope0"], 2 * b0 + t + 1)
                            pe.wait_ge(s["v_lo0"], 2 * b0 + t + 1)
                        add_row(qk_ps[1][t][:, 0:512], B_Q)
                        add_row(qk_ps[1][t][:, 512:768], B_KV)
                        product([qk_ps[1][t][:, 0:512], qk_ps[1][t][:, 512:768]], xT[1], t,
                                [(w_qkv1, 0, 512), (w_qkv1, 512, 768)], start=False).then_inc(s["proj1"], 1)
                for l, b in ((0, b0), (1, b1)):
                    if b is not None:
                        pe.wait_ge(s[f"qk_lo{l}"], 2 * b + 2)
                        pe.wait_ge(s[f"v_lo{l}"], 2 * b + 2)
                        pe.wait_ge(s[f"rope{l}"], 2 * b + 2)
                pe.wait_ge(s["cleared"], 3) if b1 is None else pe.wait_ge(s["cleared"], CLEARED(b0, b1))
                if b0 is not None:
                    pe.wait_ge(s["ffn_in"], 2 * b0 + 2)
                turn_qk(order, 0, n0)

                def used(k):
                    if k == 0:
                        return (s["mid"], 2 * b1 + 2) if b1 is not None else (s["chosenT"], b0 + 1)
                    l, g = order[k - 1]
                    return (s[f"attn{l}"], GROUPS * bs[l] + g + 1)

                for k in range(size + 3):
                    n = n0 + k
                    some = units(order, k) if b0 is not None and k < size else []

                    def experts(i, lo, hi=PRODUCTS):
                        if i < len(some):
                            expert(b0, *some[i], b1 is None, lo, hi)

                    if k < size:
                        scores(order, k, n, lambda: experts(0, 0, FIRST))
                        if k + 1 < size:
                            if chunk_after(order, k - 1) is not None:
                                j = chunk_after(order, k - 1)
                                pe.wait_ge(s[f"at_lo{order[j][0]}"], 4 * bs[order[j][0]] + order[j][1] // 2 + 1)
                            turn_qk(order, k + 1, n + 1)
                    if 2 <= k < size + 2:
                        values(order, k - 2, n - 2, bs[order[k - 2][0]], used(k - 2))
                    experts(0, FIRST, PRODUCTS if len(some) > 1 else SECOND)
                    if k < size:
                        pe.wait_ge(s["max_lo"], n + 1)
                        if k + 1 < size:
                            pe.wait_ge(s["k_t"], n + 2)
                    j = chunk_after(order, k)
                    if j is not None:
                        if k > size and chunk_after(order, k - 1) is not None:
                            i = chunk_after(order, k - 1)
                            pe.wait_ge(s[f"at_lo{order[i][0]}"], 4 * bs[order[i][0]] + order[i][1] // 2 + 1)
                        turn_chunk(order, j, bs[order[j][0]])
                    if k < size:
                        turn_q(*order[k]).then_inc(s["t2"], 1)
                    if len(some) > 1:
                        experts(1, 0)
                    else:
                        experts(0, SECOND)
                    if k < size:
                        scores_t(order, k, n)
                if b0 is not None:
                    if b1 is None:
                        pe.wait_ge(s["w_lo"], N)
                    pe.wait_ge(s["s_max"], 3 * (n0 + size))
                    for t in range(TILES):
                        pe.wait_ge(s["at_lo0"], 4 * b0 + 4)
                        product([out_ps[0][t]], aT[0], t, [(w_o0, 0, 512)]).then_inc(s["out0"], 1)
                if b1 is not None:
                    pe.wait_ge(s["at_lo1"], 4 * b1 + 4)
                    pe.wait_ge(s["mid_lo"], b1 + 1)
                    for t in range(TILES):
                        last = pe.transpose(tT[:, t * P:(t + 1) * P], mid16[:, t, :, :].rearrange("p a n -> p (a n)"), ident16[:])
                    last.then_inc(s["mid_ps"], 1)
                    pe.wait_ge(s["p32"], n0 + size)
                    for t in range(TILES):
                        add_row(out_ps[1][t], B_O)
                        product([out_ps[1][t]], aT[1], t, [(w_o1, 0, 512)], start=False).then_inc(s["out1"], 1)
                    pe.wait_ge(s["midT"], b1 + 1)
                    if b0 is not None:
                        pe.wait_ge(s["mixed"], 16 * b0 + 16)
                    for t in range(TILES):
                        for j in range(2):
                            last = pe.matmul(delta_ps[t], midT[:, t * P:(t + 1) * P], w_b[:, j, :], start=j == 0, stop=j == 1)
                        last.then_inc(s["delta"], 1)

            def CLEARED(b0, b1):
                if b0 is None:
                    return 2 + 2 * BATCH * 2
                return 2 + 2 + 4 * b0

            rounds(pe, run)


_OUT = (BATCH, SEQ, C)


def kernel(**inputs):
    import concourse.bacc as _bacc
    from concourse.bass_utils import run_bass_kernel_spmd as _run

    v = {k: np.asarray(w) for k, w in inputs.items()}
    rows = np.arange(W_QKV1).reshape(KV_HEADS, GROUP + 2, HD)
    order = np.concatenate([rows[:, :GROUP].ravel(), rows[:, GROUP].ravel(), rows[:, GROUP + 1].ravel()])
    t = np.arange(SEQ, dtype=np.float32)
    inv = (1.0 / 1000000.0 ** (np.arange(0, HD, 2, dtype=np.float32) / HD)).astype(np.float32)
    freq = np.outer(t, inv).astype(np.float32)

    def tiled(table):
        return np.ascontiguousarray(table.reshape(TILES, P, -1).transpose(1, 0, 2)).astype(np.float32)

    arrays = {
        "x": v["L0_attn_x"],
        "wqkv0": np.concatenate([v["L0_attn_wq"].T, v["L0_attn_wk"].T, v["L0_attn_wv"].T], axis=1),
        "wo0": v["L0_attn_wo"].T,
        "gate": v["L0_ffn_gate_w"].T,
        "gate_b": v["L0_ffn_gate_b"],
        "wexp": v["L0_ffn_expert_w"].reshape(-1, C).T,
        "expert_b": v["L0_ffn_expert_b"],
        "wqkv1": v["L1_attn_w_qkv"][order].T,
        "b_qkv1": v["L1_attn_b_qkv"][order][None, :],
        "wo1": v["L1_attn_w_dense"].T,
        "b_o1": v["L1_attn_b_dense"][None, :],
        "router": v["L1_ffn_router_w"].T,
        "A": v["L1_ffn_A"].reshape(-1, C).T,
        "B": v["L1_ffn_B"].transpose(0, 2, 1).reshape(-1, C),
        "ident": np.eye(P, dtype=np.float32),
        "rope0": tiled(np.stack([np.cos(t) * OUT, -np.sin(t) * OUT, np.sin(t) * OUT], axis=1)),
        "cos1": tiled(np.concatenate([np.cos(freq), np.cos(freq)], axis=1) * OUT),
        "sin1": tiled(np.concatenate([-np.sin(freq), np.sin(freq)], axis=1) * OUT),
        "iota8": np.tile(np.arange(8, dtype=np.float32), (P, 1)),
    }
    nc = _bacc.Bacc("TRN2", target_bir_lowering=False, num_devices=1)
    ins, aps = {}, {}
    for name, x in arrays.items():
        x = np.ascontiguousarray(x)
        ins["in_" + name] = x
        aps[name] = nc.dram_tensor("in_" + name, x.shape, mybir.dt.from_np(x.dtype), kind="ExternalInput").ap()
    aps["out"] = nc.dram_tensor("out", _OUT, F32, kind="ExternalOutput").ap()
    build(nc, aps)
    return _run(nc, [ins], core_ids=[0]).results[0]["out"]
```

```python
from collections import namedtuple
from contextlib import ExitStack

import numpy as np

import concourse.bass as bass
from concourse import mybir
from concourse.alu_op_type import AluOpType as ALU

F32 = mybir.dt.float32
F16 = mybir.dt.float16
BF16 = mybir.dt.bfloat16
U32 = mybir.dt.uint32
ACT = mybir.ActivationFunctionType
AX = mybir.AxisListType

BATCH, SEQ, C = 4, 256, 512
P = 128
TILES = SEQ // P
CH = C // P
HEADS, HD = 32, 16
KV_HEADS = 8
GROUP = 4
PAIRS = GROUP // 2
GROUPS = HEADS // GROUP
BLK = 64
MAXROW = 3 * HD
VW = 2 * HD + 1
PIECE = 512
EXPERTS = 8
RANK, LORA = 16, 4
LORA_SCALE = 16.0 / RANK ** 0.5
EPS = 1e-5
NEG = -1e30

PRODUCTS = 3 * CH
FIRST = 5

CONSTS = 5 * 16

XS, WS = 16.0, 128.0
OUT = 1.0 / (XS * WS)

W_QKV0, W_O0, W_EXP, W_QKV1, W_O1 = 1536, 512, EXPERTS * 512, 768, 512
ROUTER_AT = EXPERTS
A_AT = EXPERTS + 4
W_SMALL = A_AT + 64


Turn = namedtuple("Turn", "layer group seq n")


def build(nc, a):
    ctx = ExitStack()
    with ctx:
        def sb(name, shape, dt=F32):
            return ctx.enter_context(nc.sbuf_tensor(name, shape, dt))

        def ps(name, shape, dt=F32):
            return ctx.enter_context(nc.psum_tensor(name, shape, dt))

        w_qkv0 = sb("w_qkv0", [P, 2, CH, W_QKV0], F16)
        w_o0 = sb("w_o0", [P, 2, CH, W_O0], F16)
        w_exp = sb("w_exp", [P, 2, CH, W_EXP], F16)
        w_qkv1 = sb("w_qkv1", [P, 2, CH, W_QKV1], F16)
        w_o1 = sb("w_o1", [P, 2, CH, W_O1], F16)
        w_small = sb("w_small", [P, 2, CH, W_SMALL], F16)
        w_b = sb("w_b", [P, 2, 512], F16)
        B_EXP, B_O, B_Q, B_KV = 0, 32, 64, 96
        bias = sb("bias", [P, 2, 512], F16)

        ident32 = sb("ident32", [P, P])
        ident16 = sb("ident16", [P, P], F16)
        identb = sb("identb", [P, P], BF16)
        ones = sb("ones", [P, P], F16)
        mask_qk = sb("mask_qk", [P, P], BF16)
        mask_kq = sb("mask_kq", [P, P], BF16)
        rope0 = sb("rope0", [P, TILES, 3])
        cos1 = sb("cos1", [P, TILES, HD])
        sin1 = sb("sin1", [P, TILES, HD])
        gate_bias = sb("gate_bias", [P, EXPERTS])
        iota8 = sb("iota8", [P, 8])
        minus_half = sb("minus_half", [P, TILES])

        rot = sb("rot", [P, 1024])
        rot_t = rot[:].rearrange("p (t c) -> p t c", t=TILES)
        x0 = sb("x0", [P, TILES, C])
        ffn = sb("ffn", [P, TILES, C])
        th = sb("th", [P, C])
        stats = sb("stats", [P, TILES, 6])
        mv = sb("mv", [P, TILES, 2])
        var_eps = sb("var_eps", [P, TILES])
        rstd = sb("rstd", [P, TILES])
        aT = [sb(f"aT{l}", [P, 2, CH, SEQ], F16) for l in range(2)]
        xT = [sb("xT0", [P, 2, CH, SEQ], F16)[:], x0[:].rearrange("p t c -> p (t c)").bitcast(F16).rearrange(
            "p (a c n) -> p a c n", a=2, c=CH)]
        qs = [sb(f"qs{l}", [P, TILES, HEADS, BLK], F16) for l in range(2)]
        ks = [sb("ks0", [P, TILES, HEADS, BLK], F16), sb("ks1", [P, TILES, KV_HEADS, BLK], F16)]
        vs = [sb("vs0", [P, TILES, HEADS, VW], F16), sb("vs1", [P, TILES, KV_HEADS, VW], F16)]
        qT = [sb(f"qT{i}", [P, PAIRS, SEQ], F16) for i in range(2)]
        kT = [sb(f"kT{i}", [P, PAIRS, 2, SEQ], F16) for i in range(2)]
        qmT = sb("qmT", [P, PAIRS, SEQ], F16)
        neg_max = sb("neg_max", [P, TILES, GROUP])
        p32 = sb("p32", [P, 3 * 512])
        p_hi = [sb(f"p_hi{i}", [P, 3 * 512], F16) for i in range(2)]
        p_lo = sb("p_lo", [P, 3 * 512], F16)
        recip = sb("recip", [P, TILES, GROUP])
        o_sum = sb("o_sum", [P, TILES, GROUP, HD])
        attn = [sb(f"attn{l}", [P, TILES, P]) for l in range(2)]
        logits = [sb(f"logits{l}", [P, TILES, 8]) for l in range(2)]
        top = [sb(f"top{l}", [P, TILES, 8]) for l in range(2)]
        top_at = [sb(f"top_at{l}", [P, TILES, 8], U32) for l in range(2)]
        top_f = [sb(f"top_f{l}", [P, TILES, 2]) for l in range(2)]
        chosen = sb("chosen", [P, TILES, EXPERTS])
        chosen16 = sb("chosen16", [P, TILES, EXPERTS], F16)
        chosenT = sb("chosenT", [EXPERTS, SEQ], F16)
        r_bias = sb("r_bias", [P, TILES])
        r_exp = sb("r_exp", [P, TILES, LORA])
        r_sel = sb("r_sel", [P, TILES, LORA])
        r_gate = sb("r_gate", [P, TILES, LORA])
        r_sum = sb("r_sum", [P, TILES])
        r_rec = sb("r_rec", [P, TILES])
        mid16 = sb("mid16", [P, TILES, 2, LORA * RANK], F16)
        midT = sb("midT", [P, SEQ], F16)
        mid = th[:, 0:TILES * LORA * RANK].rearrange("p (t n) -> p t n", t=TILES)
        slots = [qs[1][:, t, :, :].rearrange("p h k -> p (h k)").bitcast(F32)[:, PIECE * i:PIECE * (i + 1)]
                 for t in range(TILES) for i in range(2)] + [ks[1][:].rearrange("p t h k -> p (t h k)").bitcast(F32)]

        psB = ps("psB", [P, 3, 512])
        psS = ps("psS", [P, 2, 512])
        psT = ps("psT", [P, 512])
        psO = ps("psO", [P, 512])
        psW = ps("psW", [P, 512])
        tT = psT[:, :].bitcast(F16)
        small_at = [[(8 * t, 8 * t + EXPERTS) for t in range(TILES)],
                    [((W_SMALL - ROUTER_AT) * t, (W_SMALL - ROUTER_AT) * (t + 1)) for t in range(TILES)]]
        o_ps = psO[:, 0:TILES * GROUP * VW].rearrange("p (t h v) -> p t h v", t=TILES, h=GROUP)
        both = """xn bn mv var rstd xt_ps xt_hi xt_lo proj small rope v_hi v_lo qk_hi qk_lo cleared logits top top_at top_f
            attn at_ps at_hi at_lo out th gated weighed"""
        one = """const x_rot x_in x_st x_out w_hi w_lo made cleared masks rot cosx swap
            mid_raw chosen chosen_T chosenT ffn_bias ffn_in expert mixed resid
            t1 q_t k_t s_ps s_max max_hi max_lo t2 qm_t st p32 p_hi p_lo pv recip o_lo o_sum
            r_bias r_exp r_first r_sel r_eg r_sum r_rec r_gate mid mid_hi mid_lo mid_ps midT delta v_ps ident"""
        names = one.split() + [n + l for n in both.split() for l in "01"] + [f"staged{i}" for i in range(len(slots))]
        s = {n: ctx.enter_context(nc.semaphore("s_" + n)) for n in names}
        block = ctx.enter_context(nc.Block())

        work, until = [], {}

        def weight(name, dst, src, lo, hi):
            for c in range(CH):
                for at in range(lo, hi, PIECE):
                    to = min(at + PIECE, hi)
                    work.append((dst[:, :, c, at:to], [(src[c * P:(c + 1) * P, at:to], 0, P, 0, to - at)]))
            until[name] = len(work)

        for c in range(CH):
            rows = slice(c * P, (c + 1) * P)
            work.append((w_small[:, :, c, :], [(a["gate"][rows, :], 0, P, 0, EXPERTS), (a["router"][rows, :], 0, P, ROUTER_AT, A_AT),
                                               (a["A"][rows, :], 0, P, A_AT, W_SMALL)]))
        until["small"] = len(work)
        for part in range(3):
            weight(f"qkv0_{part}", w_qkv0, a["wqkv0"], 512 * part, 512 * (part + 1))
        for at, n, name, lo, hi in ((B_EXP, EXPERTS, "expert_b", 0, 512), (B_O, 1, "b_o1", 0, 512), (B_Q, 1, "b_qkv1", 0, 512),
                                    (B_KV, 1, "b_qkv1", 512, 768)):
            work.append((bias[at:at + n, :, 0:hi - lo], [(a[name][:, lo:hi], at, at + n, 0, hi - lo)]))
        until["bias"] = len(work)
        for e in range(EXPERTS):
            weight(f"exp{e}", w_exp, a["wexp"], 512 * e, 512 * (e + 1))
        weight("o0", w_o0, a["wo0"], 0, W_O0)
        weight("qkv1", w_qkv1, a["wqkv1"], 0, W_QKV1)
        weight("o1", w_o1, a["wo1"], 0, W_O1)
        work.append((w_b[:, :, :], [(a["B"], 0, 64, 0, 512), (a["B"], 64, P, 0, 512)]))
        N = len(work)
        landed, landed_by = [0] * len(slots), []
        for i, (_, parts) in enumerate(work):
            landed[i % len(slots)] += 16 * len(parts)
            landed_by.append(landed[i % len(slots)])
        split_by = [until["exp1"]]
        while split_by[-1] < until["exp7"]:
            split_by.append(split_by[-1] + 2)
        while len(split_by) < 2 * GROUPS + 1:
            split_by.append(min(N, split_by[-1] + 3))

        def staged(i):
            return s[f"staged{i % len(slots)}"]

        class Pieces:
            count = 0

            def until(self, up_to):
                lo, self.count = self.count, max(self.count, up_to)
                return range(lo, self.count)

        def piece(i):
            dst, parts = work[i]
            return dst, slots[i % len(slots)][parts[0][1]:parts[-1][2], 0:parts[-1][4]]

        def heads(x, lo, hi):
            return x[:, lo:hi].rearrange("p (h d) -> p h d", d=HD)

        def stacks(l, b):
            at = 0 if isinstance(b, int) and b == BATCH - 1 else l
            return (qs[at], ks[at][:, :, 0:HEADS if l == 0 else KV_HEADS, :], vs[at][:, :, 0:HEADS if l == 0 else KV_HEADS, :])

        def input_t(l, b):
            return xT[0 if isinstance(b, int) and b == BATCH - 1 else l]

        def turns(l, b, n0):
            return [Turn(l, g, b, n0 + g) for g in range(GROUPS)]

        def experts(b, lo, hi):
            return [("expert", b, *divmod(u, TILES)) for u in range(lo, hi)]

        def beside_first(b):
            E, c = experts(b, 0, 10), b - 1
            end1 = [[], [], [], []]
            if not (isinstance(b, int) and b == 1):
                end1 = [[("delta", b - 2, 0)], [("out1", b - 2, 0)], [("delta", b - 2, 1)], [("out1", b - 2, 1), ("add", b - 2)]]
            return [[[("turn", 1, c, 0)], [("turn", 1, c, 1)], [("bias", b, 0), ("bias", b, 1)]],
                    [[E[0]], [("small", 1, c)], [E[1]]],
                    [[E[2]], [("choose", 1, c), ("proj", 1, c, 0, 0)], [("proj", 1, c, 0, 1)]],
                    [[E[3]], [("proj", 1, c, 1, 0)], [E[4]]],
                    [[E[5]], [("proj", 1, c, 1, 1)], []],
                    [[E[6]], end1[0], end1[1]],
                    [[E[7]], end1[2], end1[3]],
                    [[E[8]], [E[9]], [("mid", c)]]]

        def beside_second(b):
            E, c = experts(b, 10, 16), b + 1
            return [[[E[0]], [E[1]], []],
                    [[E[2]], [("stats", c), E[3]], [("var", c)]],
                    [[E[4]], [E[5]], [("norm", c)]],
                    [[("turn", 0, c, 0)], [("turn", 0, c, 1), ("gate", b)], [("small", 0, c)]],
                    [[("choose", 0, c), ("proj", 0, c, 0, 0)], [("proj", 0, c, 0, 1)], [("out0", b, 0)]],
                    [[("resid", b, 0), ("proj", 0, c, 1, 0)], [("proj", 0, c, 1, 1)], [("out0", b, 1)]],
                    [[("resid", b, 1), ("proj", 0, c, 0, 2)], [("norm1", b), ("chosen", c)], []],
                    [[("proj", 0, c, 1, 2)], [], []]]

        last = BATCH - 1
        E = experts(last, 10, 16)
        beside_last_but_one = [
            [[E[0]], [E[1]], []], [[E[2]], [E[3]], []], [[E[4]], [E[5]], [("gate", last)]],
            [[("out0", last, 0)], [("out0", last, 1), ("resid", last, 0), ("resid", last, 1)], [("norm1", last)]],
            [[], [("turn", 1, last, 0)], [("turn", 1, last, 1)]],
            [[("small", 1, last)], [("choose", 1, last), ("proj", 1, last, 0, 0)], [("proj", 1, last, 0, 1)]],
            [[("proj", 1, last, 1, 0)], [("proj", 1, last, 1, 1)], []], [[], [], []]]
        beside_last = [[[], [], []], [[], [], []], [[], [], [("delta", last - 1, 0)]],
                       [[("out1", last - 1, 0)], [("delta", last - 1, 1)], [("out1", last - 1, 1), ("add", last - 1)]],
                       [[("mid", last)], [], []]] + [[[], [], []]] * 3
        E = experts(0, 0, 16)
        beside_very_first = [[[E[2 * k]], [E[2 * k + 1]], []] for k in range(GROUPS)]
        for k, kind in ((4, "stats"), (5, "var"), (6, "norm")):
            beside_very_first[k][2] = [(kind, 1)]
        start = [("weights", until["small"]), ("turn", 0, 0, 0), ("turn", 0, 0, 1), ("small", 0, 0), ("weights", until["qkv0_2"]),
                 ("proj", 0, 0, 0, 0), ("weights", until["bias"]), ("choose", 0, 0), ("stack", 0, 0, 0, 0), ("proj", 0, 0, 0, 1), ("proj", 0, 0, 0, 2),
                 ("stack", 0, 0, 0, 1), ("weights", until["bias"] + 1), ("proj", 0, 0, 1, 0), ("weights", until["exp0"] - 1),
                 ("stack", 0, 0, 1, 0), ("proj", 0, 0, 1, 1), ("weights", until["exp0"] + 1), ("stack", 0, 0, 1, 1),
                 ("proj", 0, 0, 1, 2), ("chosen", 0), ("bias", 0, 0), ("bias", 0, 1),
                 ("weights", until["exp1"])]
        beside_very_first += [[[], [], [("turn", 0, 1, 0), ("turn", 0, 1, 1), ("small", 0, 1), ("choose", 0, 1), ("proj", 0, 1, 0, 0),
                                       ("weights", N - 6), ("stack", 0, 1, 0, 0), ("proj", 0, 1, 0, 1)]],
                              [[], [], [("proj", 0, 1, 0, 2), ("stack", 0, 1, 0, 1), ("weights", N), ("proj", 0, 1, 1, 0)]],
                              [[], [], [("stack", 0, 1, 1, 0), ("proj", 0, 1, 1, 1), ("gate", 0), ("stack", 0, 1, 1, 1), ("out0", 0, 0),
                                       ("resid", 0, 0), ("out0", 0, 1)]]]
        between = [("resid", 0, 1), ("norm1", 0), ("proj", 0, 1, 1, 2), ("chosen", 1)]
        beside_last.append([[], [], [("delta", last, 0)]])
        end = [("out1", last, 0), ("delta", last, 1), ("out1", last, 1), ("add", last)]

        def with_stacks(jobs):
            out = []
            for x in jobs:
                out.append(x)
                if x[0] == "proj" and x[4] < 2:
                    out.append(("stack", *x[1:]))
            return out

        bank_of = [psW[:], psS[:, 0, :], psS[:, 1, :]]

        def on_pe(x):
            return x[0] not in ("stats", "var", "norm", "norm1", "gate", "add", "weights", "stack", "resid", "choose")

        def banked(jobs, order):
            out, i = [], 0
            for x in jobs:
                out.append((order[i % len(order)], *x))
                i += on_pe(x)
            return out

        def placed(these, jobs):
            out = []
            for x, beside in zip(these, jobs):
                first, second, third = (with_stacks(y) for y in beside)
                second = [y for y in first if y[0] == "stack"] + second
                first = [y for y in first if y[0] != "stack"]
                k = x.group % 2
                n = sum(on_pe(y) for y in second + third)
                rest = banked(second + third, (2 - k, 0) if n == 2 else (2 - k, 1 + k, 0))
                out.append([banked(first, (0,)), rest[:len(second)], rest[len(second):]])
            return out + [[[], [], banked(third, (0, 1, 2))] for _, _, third in jobs[len(these):]]

        def program(eng, job, run):
            for x in banked(start, (0, 1, 2)):
                job(*x)
            run([], turns(0, 0, 0), None, beside_very_first, True)
            for x in banked(between, (0, 1, 2)):
                job(*x)
            second = turns(0, 1, GROUPS)
            run([], second, Turn(1, 0, 0, 2 * GROUPS), beside_first(1))
            with eng.Fori(1, BATCH - 1) as b:
                before = [Turn(0, g, b, 16 * b - 8 + g) for g in range(4, GROUPS)]
                both = turns(1, b - 1, 16 * b) + turns(0, b + 1, 16 * b + 8)
                run(before, both, Turn(1, 0, b, 16 * b + 16), beside_second(b) + beside_first(b + 1))
            before = turns(0, last, 40)[4:]
            both = turns(1, last - 1, 48) + turns(1, last, 56)
            run(before, both, None, beside_last_but_one + beside_last)
            for x in banked(end, (0, 1, 2)):
                job(*x)

        def rotated(b):
            return 4 * min(b + 2, BATCH) if isinstance(b, int) else 4 * b + 8

        def in_flight(before, these, after):
            def turn(k):
                if k < 0:
                    return before[k + len(before)] if k + len(before) >= 0 else None
                if k < len(these):
                    return these[k]
                return after if k == len(these) else None
            return turn, len(these) + (0 if after is not None else 3)

        def positive(n):
            return not isinstance(n, int) or n > 0

        def chunked(x):
            return x is not None and x.group % 2 == 1

        def seq(name, b):
            if isinstance(b, int):
                return a[name][b].rearrange("(t p) c -> p t c", p=P)
            return a[name][bass.ds(b, 1)].rearrange("b (t p) c -> p (b t) c", p=P)

        @block.sync
        def _(sp):
            sp.dma_start(ident32[:], a["ident"]).then_inc(s["ident"], 16)
            sp.dma_start(rot_t, seq("x", 0)).then_inc(s["x_rot"], 16)

            def load(lo, hi):
                for i in range(lo, hi):
                    if i >= len(slots):
                        sp.wait_ge(s["w_lo"], i - len(slots) + 1)
                    for src, p0, p1, c0, c1 in work[i][1]:
                        sp.dma_start(slots[i % len(slots)][p0:p1, c0:c1], src).then_inc(staged(i), 16)

            def x_for_norm(b):
                sp.dma_start(rot_t, seq("x", b)).then_inc(s["x_rot"], 16)

            def x_for_sum(b):
                sp.dma_start(x0[:], seq("x", b)).then_inc(s["x_in"], 16)

            def store(b):
                sp.wait_ge(s["resid"], 2 * b + 2)
                sp.dma_start(seq("out", b), x0[:]).then_inc(s["x_st"], 16)

            load(0, until["exp2"])
            x_for_sum(0)
            sp.wait_ge(s["qk_lo0"], 4)
            x_for_norm(1)
            load(until["exp2"], N)
            store(0)
            sp.wait_ge(s["proj1"], 4)
            x_for_sum(1)
            with sp.Fori(1, BATCH - 1) as b:
                following = sp.snap(b + 1)
                sp.wait_ge(s["qk_lo1"], 4 * b)
                x_for_norm(following)
                store(b)
                sp.wait_ge(s["x_out"], 16 * b)
                x_for_sum(following)
            store(last)

        @block.gpsimd
        def _(pool):
            pool.memset(mask_qk[:], 0.0).then_inc(s["masks"], 1)
            pool.memset(mask_kq[:], 0.0).then_inc(s["masks"], 1)
            pool.memset(minus_half[:], -0.5).then_inc(s["masks"], 1)
            pool.wait_ge(s["masks"], 3)
            pool.affine_select(out=mask_qk[:], in_=mask_qk[:], compare_op=ALU.is_ge, fill=NEG, base=0,
                               pattern=[[-1, P]], channel_multiplier=1).then_inc(s["masks"], 1)
            pool.affine_select(out=mask_kq[:], in_=mask_kq[:], compare_op=ALU.is_ge, fill=NEG, base=0,
                               pattern=[[1, P]], channel_multiplier=-1).then_inc(s["masks"], 1)

            def clear(l):
                for t in range(TILES):
                    pool.memset(ks[l][:, t, :, MAXROW:MAXROW + 2], 1.0)
                    pool.memset(ks[l][:, t, :, MAXROW + 2:BLK], 0.0)
                    last = pool.memset(qs[l][:, t, :, MAXROW + 2:BLK], 0.0)
                last.then_inc(s[f"cleared{l}"], 1)

            clear(0)

            def rms(l, m):
                pool.wait_ge(s[f"var{l}"], m + 1)
                pool.tensor_tensor(rstd[:], var_eps[:], minus_half[:], ALU.pow).then_inc(s[f"rstd{l}"], 1)

            def job(_, kind, *at):
                if kind == "weights" and at[0] == N:
                    pool.wait_ge(s["w_lo"], N)
                    clear(1)
                elif kind == "var":
                    rms(0, at[0])
                elif kind == "norm1":
                    rms(1, at[0])
                elif kind == "stack":
                    l, b, t, part = at
                    q, k, _ = stacks(l, b)
                    pool.wait_ge(s[f"qk_hi{l}"], 4 * b + 2 * t + part + 1)
                    if part == 0:
                        pool.tensor_tensor(q[:, t, :, HD:2 * HD], heads(rot, 0, 512), q[:, t, :, 0:HD],
                                           ALU.subtract).then_inc(s[f"qk_lo{l}"], 1)
                        pool.memset(q[:, t, :, MAXROW:MAXROW + 2], 0.0).then_inc(s[f"cleared{l}"], 1)
                    else:
                        pool.tensor_tensor(k[:, t, :, 2 * HD:3 * HD], heads(rot, 512, 1024 if l == 0 else 640), k[:, t, :, 0:HD],
                                           ALU.subtract).then_inc(s[f"qk_lo{l}"], 1)
                elif kind == "add":
                    b, = at
                    pool.wait_ge(s["x_st"], 16 * b + 16)
                    pool.wait_ge(s["weighed1"], 2 * b + 2)
                    pool.dma_start(seq("out", b), rot_t, accum_op=ALU.add).then_inc(s["x_out"], 16)

            def run(before, these, after, jobs, first=False):
                turn, count = in_flight(before, these, after)
                jobs = placed(these, jobs)
                for k in range(count):
                    if turn(k - 1) is not None:
                        n = turn(k - 1).n
                        pool.wait_ge(s["p32"], n + 1)
                        pool.wait_ge(s["pv"], n)
                        pool.tensor_tensor(p_lo[:], p32[:], p_hi[turn(k - 1).group % 2][:], ALU.subtract).then_inc(s["p_lo"], 1)
                    for x in sum(jobs[k], []) if k < len(jobs) else []:
                        job(*x)

            rms(0, 0)
            program(pool, job, run)
            pool.wait_ge(s["x_out"], BATCH * 16)
            pool.wait_ge(s["x_st"], BATCH * 16)

        @block.scalar
        def _(act):
            done = Pieces()

            def split(up_to):
                for i in done.until(up_to):
                    act.wait_ge(staged(i), landed_by[i])
                    dst, src = piece(i)
                    act.activation(dst[:, 0, :], src, ACT.Copy, scale=WS).then_inc(s["w_hi"], 1)

            def job(bank, kind, *at):
                ps = bank_of[bank]
                half = ps.bitcast(F16)
                if kind == "weights":
                    split(*at)
                if kind == "turn":
                    l, b, t = at
                    if l == 1 and input_t(l, b) is xT[1]:
                        act.wait_ge(s["x_st"], 16 * b + 16)
                    act.wait_ge(s[f"xt_ps{l}"], 2 * b + t + 1)
                    act.activation(input_t(l, b)[:, 0, :, t * P:(t + 1) * P], ps.rearrange("p (c n) -> p c n", c=CH),
                                   ACT.Copy, scale=XS).then_inc(s[f"xt_hi{l}"], 1)
                elif kind == "proj":
                    l, b, t, part = at
                    v = stacks(l, b)[2]
                    w = 512 if l == 0 or part == 0 else 128
                    m = 4 * b + 2 * t + part
                    if l == 0 and part == 2 or l == 1 and part == 1:
                        act.wait_ge(s["v_ps"], 2 * b + t + 1) if l == 0 else act.wait_ge(s["proj1"], m + 1)
                        if isinstance(b, int) and b < 2:
                            used = GROUPS * b if l == 0 else 0
                        elif l == 0:
                            used = 16 * b - 16
                        else:
                            used = 48 if isinstance(b, int) else 16 * b + 8
                        if positive(used):
                            act.wait_ge(s["pv"], used)
                        at_v = 128 if l == 1 else 0
                        act.activation(v[:, t, :, 0:HD], heads(ps, at_v, at_v + w), ACT.Copy, scale=OUT).then_inc(s[f"v_hi{l}"], 1)
                    if l == 0 and part < 2:
                        act.wait_ge(s["proj0"], m + 1)
                        if t:
                            act.wait_ge(s["qk_lo0"], m - 1)
                        src2 = ps.rearrange("p (n two) -> p n two", two=2)
                        dst2 = rot[:, 512 * part:512 * (part + 1)].rearrange("p (n two) -> p n two", two=2)
                        act.activation(dst2[:, :, 0], src2[:, :, 1], ACT.Copy, scale=rope0[:, t, 1:2])
                        act.activation(dst2[:, :, 1], src2[:, :, 0], ACT.Copy, scale=rope0[:, t, 2:3]).then_inc(s["rot"], 1)
                elif kind == "stack":
                    l, b, t, part = at
                    w = 512 if l == 0 or part == 0 else 128
                    act.wait_ge(s[f"rope{l}"], 4 * b + 2 * t + part + 1)
                    for j in ((2, 0) if part == 0 else (0, 1)):
                        last_ = act.activation(stacks(l, b)[part][:, t, :, j * HD:(j + 1) * HD],
                                               heads(rot, 512 * part, 512 * part + w), ACT.Copy)
                    last_.then_inc(s[f"qk_hi{l}"], 1)
                elif kind == "chosen":
                    b, = at
                    act.wait_ge(s["chosen_T"], b + 1)
                    act.activation(chosenT[:], half[0:EXPERTS, 0:SEQ], ACT.Copy, scale=XS).then_inc(s["chosenT"], 1)
                elif kind == "bias":
                    b, t = at
                    act.wait_ge(s["ffn_bias"], 2 * b + t + 1)
                    act.activation(ffn[:, t, :], ps, ACT.Copy).then_inc(s["ffn_in"], 1)
                elif kind == "choose" and at[0] == 1:
                    b = at[1]
                    act.wait_ge(s["r_bias"], b + 1)
                    for t in range(TILES):
                        last_ = act.activation(r_exp[:, t, :], logits[1][:, t, 0:LORA], ACT.Exp, bias=r_bias[:, t:t + 1])
                    last_.then_inc(s["r_exp"], 1)
                elif kind == "gate":
                    b, = at
                    act.wait_ge(s["mixed"], 16 * b + 16)
                    for t in range(TILES):
                        if t:
                            act.wait_ge(s["gated0"], 2 * b + 1)
                        act.activation(th[:], ffn[:, t, :], ACT.Tanh, scale=0.5 * OUT).then_inc(s["th0"], 1)
                elif kind == "mid":
                    b, = at
                    act.wait_ge(s["mid_ps"], b + 1)
                    act.activation(midT[:], half[:, 0:SEQ], ACT.Copy).then_inc(s["midT"], 1)
                elif kind == "delta":
                    b, t = at
                    act.wait_ge(s["delta"], 2 * b + t + 1)
                    if t:
                        act.wait_ge(s["weighed1"], 2 * b + 1)
                    else:
                        act.wait_ge(s["rope1"], rotated(b))
                        if isinstance(b, int) and b == last:
                            act.wait_ge(s["weighed1"], 2 * b)
                    act.activation(th[:], ps, ACT.Tanh, scale=0.5 * OUT).then_inc(s["th1"], 1)

            def q_turned(n):
                act.wait_ge(s["t1"], n + 1)
                return tT[:, 0:PAIRS * SEQ].rearrange("p (j n) -> p j n", j=PAIRS)

            def softmax(x, part):
                n = x.n
                scale = HD ** -0.5 if x.layer == 0 else 1.0 / HD
                src = psB[:].rearrange("p a n -> p (a n)")
                if part == 0:
                    act.wait_ge(s["st"], n + 1)
                    if positive(n - 1):
                        act.wait_ge(s["pv"], n - 1)
                    act.activation(p_hi[x.group % 2][:], src, ACT.Exp, scale=scale).then_inc(s["p_hi"], 1)
                else:
                    act.wait_ge(s["p_lo"], n)
                    act.activation(p32[:], src, ACT.Exp, scale=scale).then_inc(s["p32"], 1)

            def chunk_hi(x):
                l, c = x.layer, x.group // 2
                act.wait_ge(s[f"at_ps{l}"], 4 * x.seq + c + 1)
                act.activation(aT[l][:, 0, c, :], psT[:, SEQ:2 * SEQ], ACT.Copy, scale=XS).then_inc(s[f"at_hi{l}"], 1)

            def turned(x):
                act.activation(qT[x.group % 2][:], q_turned(x.n), ACT.Copy).then_inc(s["q_t"], 1)

            def run(before, these, after, jobs, first=False):
                turn, count = in_flight(before, these, after)
                jobs = placed(these, jobs)
                if not before:
                    turned(these[0])
                for k in range(count):
                    mine = jobs[k] if k < len(jobs) else [[], [], []]
                    if turn(k - 1) is not None:
                        softmax(turn(k - 1), 0)
                    if turn(k) is not None and turn(k + 1) is not None:
                        turned(turn(k + 1))
                    if turn(k - 1) is not None:
                        softmax(turn(k - 1), 1)
                    for x in mine[0]:
                        job(*x)
                    if first and k < GROUPS:
                        split(split_by[2 * k + 1])
                    if turn(k) is not None:
                        act.wait_ge(s["t2"], turn(k).n + 1)
                        act.activation(qmT[:], tT[:, 0:PAIRS * SEQ].rearrange("p (j n) -> p j n", j=PAIRS), ACT.Copy).then_inc(s["qm_t"], 1)
                    if chunked(turn(k - 3)):
                        chunk_hi(turn(k - 3))
                    for x in mine[1]:
                        job(*x)
                    if first and k < GROUPS:
                        split(split_by[2 * k + 2])
                    for x in mine[2]:
                        job(*x)

            for dst, src in ((rope0, "rope0"), (cos1, "cos1"), (sin1, "sin1"), (iota8, "iota8")):
                act.dma_start(dst[:], a[src]).then_inc(s["const"], 16)
            act.dma_start(gate_bias[:], a["gate_b"].partition_broadcast(P)).then_inc(s["const"], 16)
            act.wait_ge(s["const"], CONSTS)
            act.wait_ge(s["cleared0"], 1)
            program(act, job, run)

        @block.vector
        def _(dve):
            def wait_alone(name, value):
                if not isinstance(value, int):
                    value = dve.snap(value)
                dve.wait_ge(s["const"], CONSTS)
                dve.wait_ge(s[name], value)

            done = Pieces()

            def split(up_to):
                for i in done.until(up_to):
                    dst, src = piece(i)
                    dve.wait_ge(s["w_hi"], i + 1)
                    dve.scalar_tensor_tensor(out=dst[:, 1, :], in0=src, scalar=WS, in1=dst[:, 0, :],
                                             op0=ALU.mult, op1=ALU.subtract).then_inc(s["w_lo"], 1)

            def norm_stats(l, b, t):
                dve.bn_stats(stats[:, t, :], (rot_t, x0)[l][:, t, :]).then_inc(s[f"bn{l}"], 1)

            def norm_var(l, b):
                dve.wait_ge(s[f"bn{l}"], 2 * b + 2)
                dve.memset(var_eps[:], EPS)
                for t in range(TILES):
                    dve.bn_aggr(mv[:, t, :], stats[:, t, :]).then_inc(s[f"mv{l}"], 1)
                dve.wait_ge(s[f"mv{l}"], 2 * b + 2)
                dve.tensor_tensor(var_eps[:], mv[:, :, 1], var_eps[:], ALU.add).then_inc(s[f"var{l}"], 1)

            def norm_x(l, b, t):
                dve.wait_ge(s[f"rstd{l}"], b + 1)
                dve.tensor_scalar((rot_t, ffn)[l][:, t, :], (rot_t, x0)[l][:, t, :], mv[:, t, 0:1], rstd[:, t:t + 1],
                                  ALU.subtract, ALU.mult).then_inc(s[f"xn{l}"], 1)

            def largest(l, b):
                wait_alone(f"logits{l}", 2 * b + 2)
                for t in range(TILES):
                    dve.max(top[l][:, t, :], logits[l][:, t, :]).then_inc(s[f"top{l}"], 1)
                wait_alone(f"top{l}", 2 * b + 2)
                for t in range(TILES):
                    dve.max_index(top_at[l][:, t, :], top[l][:, t, :], logits[l][:, t, :]).then_inc(s[f"top_at{l}"], 1)
                dve.wait_ge(s[f"top_at{l}"], 2 * b + 2)
                dve.tensor_copy(top_f[l][:], top_at[l][:, :, 0:2]).then_inc(s[f"top_f{l}"], 1)

            def gate_logits(b, ps):
                dve.wait_ge(s["small0"], b + 1)
                for t in range(TILES):
                    lo, hi = small_at[0][t]
                    dve.scalar_tensor_tensor(out=logits[0][:, t, :], in0=ps[:, lo:hi], scalar=OUT,
                                             in1=gate_bias[:], op0=ALU.mult, op1=ALU.add).then_inc(s["logits0"], 1)

            def choose(b):
                largest(0, b)
                dve.wait_ge(s["top_f0"], b + 1)
                for t in range(TILES):
                    dve.tensor_scalar(chosen[:, t, :], iota8[:], top_f[0][:, t, 0:1], None, ALU.is_equal)
                    last = dve.tensor_scalar(chosen16[:, t, :], iota8[:], top_f[0][:, t, 0:1], None, ALU.is_equal)
                last.then_inc(s["chosen"], 1)

            def router_logits(b, ps):
                dve.wait_ge(s["small1"], b + 1)
                for t in range(TILES):
                    lo = small_at[1][t][0]
                    dve.tensor_scalar(logits[1][:, t, 0:LORA], ps[:, lo:lo + LORA], OUT, None, ALU.mult).then_inc(s["logits1"], 1)
                for t in range(TILES):
                    lo, hi = small_at[1][t]
                    dve.tensor_copy(mid[:, t, :], ps[:, lo + LORA:hi]).then_inc(s["mid_raw"], 1)

            def route(b):
                largest(1, b)
                dve.tensor_scalar(r_bias[:], top[1][:, :, 0], -1.0, None, ALU.mult).then_inc(s["r_bias"], 1)
                dve.wait_ge(s["top_f1"], b + 1)
                for t in range(TILES):
                    dve.tensor_scalar(r_sel[:, t, :], iota8[:, 0:LORA], top_f[1][:, t, 0:1], None, ALU.is_equal).then_inc(s["r_first"], 1)
                dve.wait_ge(s["r_first"], 2 * b + 2)
                for t in range(TILES):
                    dve.scalar_tensor_tensor(out=r_sel[:, t, :], in0=iota8[:, 0:LORA], scalar=top_f[1][:, t, 1:2], in1=r_sel[:, t, :],
                                             op0=ALU.is_equal, op1=ALU.add).then_inc(s["r_sel"], 1)
                dve.wait_ge(s["r_sel"], 2 * b + 2)
                dve.wait_ge(s["r_exp"], b + 1)
                dve.tensor_tensor(r_exp[:], r_exp[:], r_sel[:], ALU.mult).then_inc(s["r_eg"], 1)
                dve.wait_ge(s["r_eg"], b + 1)
                dve.tensor_reduce(r_sum[:], r_exp[:], AX.X, ALU.add).then_inc(s["r_sum"], 1)
                dve.wait_ge(s["r_sum"], b + 1)
                dve.reciprocal(r_rec[:], r_sum[:]).then_inc(s["r_rec"], 1)
                dve.wait_ge(s["r_rec"], b + 1)
                for t in range(TILES):
                    dve.tensor_scalar(r_gate[:, t, :], r_exp[:, t, :], r_rec[:, t:t + 1], LORA_SCALE * OUT * XS,
                                      ALU.mult, ALU.mult).then_inc(s["r_gate"], 1)
                dve.wait_ge(s["r_gate"], 2 * b + 2)
                dve.wait_ge(s["mid_raw"], 2 * b + 2)
                for t in range(TILES):
                    each = mid[:, t, :].rearrange("p (e r) -> p e r", e=LORA)
                    dve.tensor_tensor(each, each,
                                      r_gate[:, t, :].unsqueeze(2).broadcast_to([P, LORA, RANK]), ALU.mult).then_inc(s["mid"], 1)
                dve.wait_ge(s["mid"], 2 * b + 2)
                dve.tensor_copy(mid16[:, :, 0, :], mid[:]).then_inc(s["mid_hi"], 1)
                dve.wait_ge(s["mid_hi"], b + 1)
                dve.tensor_tensor(mid16[:, :, 1, :], mid[:], mid16[:, :, 0, :], ALU.subtract).then_inc(s["mid_lo"], 1)

            def job(bank, kind, *at):
                ps = bank_of[bank]
                if kind == "weights":
                    split(*at)
                if kind == "stats":
                    b, = at
                    dve.wait_ge(s["x_rot"], 16 * b + 16)
                    for t in range(TILES):
                        norm_stats(0, b, t)
                elif kind == "var":
                    norm_var(0, *at)
                elif kind == "norm":
                    for t in range(TILES):
                        norm_x(0, at[0], t)
                elif kind == "norm1":
                    norm_var(1, *at)
                    for t in range(TILES):
                        norm_x(1, at[0], t)
                elif kind == "turn":
                    l, b, t = at
                    tok = slice(t * P, (t + 1) * P)
                    dve.wait_ge(s[f"xt_hi{l}"], 2 * b + t + 1)
                    dve.scalar_tensor_tensor(out=input_t(l, b)[:, 1, :, tok], in0=ps.rearrange("p (c n) -> p c n", c=CH), scalar=XS,
                                             in1=input_t(l, b)[:, 0, :, tok], op0=ALU.mult, op1=ALU.subtract).then_inc(s[f"xt_lo{l}"], 1)
                elif kind == "small":
                    (gate_logits, router_logits)[at[0]](at[1], ps)
                elif kind == "choose":
                    (choose, route)[at[0]](at[1])
                elif kind == "proj":
                    l, b, t, part = at
                    v = stacks(l, b)[2]
                    m = 4 * b + 2 * t + part
                    if l == 0 and part < 2:
                        dst = rot[:, 512 * part:512 * (part + 1)]
                        dve.wait_ge(s["rot"], m + 1)
                        dve.scalar_tensor_tensor(out=dst, in0=ps, scalar=rope0[:, t, 0:1], in1=dst,
                                                 op0=ALU.mult, op1=ALU.add).then_inc(s["rope0"], 1)
                    if l == 0 and part == 2 or l == 1 and part == 1:
                        at_v = 128 if l == 1 else 0
                        dve.wait_ge(s[f"v_hi{l}"], 2 * b + t + 1)
                        dve.scalar_tensor_tensor(out=v[:, t, :, HD + 1:VW], in0=heads(ps, at_v, at_v + (512 if l == 0 else 128)),
                                                 scalar=OUT, in1=v[:, t, :, 0:HD], op0=ALU.mult, op1=ALU.subtract).then_inc(s[f"v_lo{l}"], 1)
                    if l == 1:
                        n_h, half = (HEADS, KV_HEADS)[part], HD // 2
                        w = HD * n_h
                        dst = heads(rot, 512 * part, 512 * part + w)
                        dve.wait_ge(s["proj1"], m + 1)
                        if t:
                            dve.wait_ge(s["qk_lo1"], m - 1)
                        elif isinstance(b, int) and b in (0, last):
                            dve.wait_ge(s["qk_lo0"], 8 if b == 0 else 16)
                        else:
                            dve.wait_ge(s["qk_lo0"], 4 * b + 8)
                        for lo in (0, half):
                            hi = half - lo
                            last_ = dve.tensor_tensor(dst[:, :, lo:lo + half], heads(ps, 0, w)[:, :, hi:hi + half],
                                                      sin1[:, t, lo:lo + half].unsqueeze(1).broadcast_to([P, n_h, half]), ALU.mult)
                        last_.then_inc(s["swap"], 1)
                        dve.wait_ge(s["mid_lo"], b + 1) if not (t or part) else dve.wait_ge(s["rope1"], m)
                        dve.tensor_tensor(heads(th, 0, w), heads(ps, 0, w),
                                          cos1[:, t, :].unsqueeze(1).broadcast_to([P, n_h, HD]), ALU.mult).then_inc(s["cosx"], 1)
                        dve.wait_ge(s["swap"], m + 1)
                        dve.wait_ge(s["cosx"], m + 1)
                        dve.tensor_tensor(rot[:, 512 * part:512 * part + w], th[:, 0:w], rot[:, 512 * part:512 * part + w],
                                          ALU.add).then_inc(s["rope1"], 1)
                elif kind == "expert":
                    mix(*at, ps)
                elif kind == "gate":
                    b, = at
                    for t in range(TILES):
                        dve.wait_ge(s["th0"], 2 * b + t + 1)
                        dve.scalar_tensor_tensor(out=ffn[:, t, :], in0=th[:], scalar=1.0, in1=ffn[:, t, :],
                                                 op0=ALU.add, op1=ALU.mult).then_inc(s["gated0"], 1)
                elif kind == "out0":
                    b, t = at
                    m = 2 * b + t
                    dve.wait_ge(s["gated0"], m + 1)
                    dve.wait_ge(s["out0"], m + 1)
                    dve.scalar_tensor_tensor(out=ffn[:, t, :], in0=ps, scalar=0.5 * OUT * OUT, in1=ffn[:, t, :],
                                             op0=ALU.mult, op1=ALU.mult).then_inc(s["weighed0"], 1)
                elif kind == "resid":
                    b, t = at
                    m = 2 * b + t
                    dve.wait_ge(s["weighed0"], m + 1)
                    dve.wait_ge(s["x_in"], 16 * b + 16)
                    dve.tensor_tensor(x0[:, t, :], x0[:, t, :], ffn[:, t, :], ALU.add).then_inc(s["resid"], 1)
                    dve.wait_ge(s["resid"], m + 1)
                    norm_stats(1, b, t)
                elif kind == "delta":
                    b, t = at
                    dve.wait_ge(s["th1"], 2 * b + t + 1)
                    dve.scalar_tensor_tensor(out=th[:], in0=th[:], scalar=1.0, in1=ps,
                                             op0=ALU.add, op1=ALU.mult).then_inc(s["gated1"], 1)
                elif kind == "out1":
                    b, t = at
                    m = 2 * b + t
                    dve.wait_ge(s["gated1"], m + 1)
                    dve.wait_ge(s["qk_lo1"], rotated(b))
                    if isinstance(b, int) and b == last:
                        dve.wait_ge(s["x_out"], 16 * b)
                    dve.wait_ge(s["out1"], m + 1)
                    dve.scalar_tensor_tensor(out=rot_t[:, t, :], in0=ps, scalar=0.5 * OUT * OUT, in1=th[:],
                                             op0=ALU.mult, op1=ALU.mult).then_inc(s["weighed1"], 1)

            def k_turned(x):
                dve.wait_ge(s["q_t"], x.n + 1)
                w, par = PAIRS if x.layer == 0 else 1, x.group % 2
                src = tT[:, PAIRS * SEQ:(PAIRS + w) * SEQ].rearrange("p (j n) -> p j n", j=w)
                dve.tensor_copy(kT[par][0:64, 0:w, 0, :], src[0:64])
                dve.tensor_copy(kT[par][64:P, 0:w, 1, :], src[64:P]).then_inc(s["k_t"], 1)

            def maxima(x):
                n, k = x.n, x.group
                for j in range(3):
                    dve.wait_ge(s["s_ps"], 3 * n + j + 1)
                    if j == 0:
                        out, src = neg_max[:, 0, :], psS[:, k % 2, :].rearrange("p (h k) -> p h k", h=GROUP)
                    else:
                        out = neg_max[:, 1, PAIRS * (j - 1):PAIRS * j]
                        src = psS[:, (k + j) % 2, :].rearrange("p (h k) -> p h k", h=PAIRS)
                    dve.tensor_reduce(out, src, AX.X, ALU.max, negate=True).then_inc(s["s_max"], 1)

            def max_rows(x):
                n, q = x.n, stacks(x.layer, x.seq)[0]
                at = slice(GROUP * x.group, GROUP * (x.group + 1))
                dve.wait_ge(s["s_max"], 3 * n + 3)
                dve.tensor_copy(q[:, :, at, MAXROW], neg_max[:]).then_inc(s["max_hi"], 1)
                dve.wait_ge(s["max_hi"], n + 1)
                dve.tensor_tensor(q[:, :, at, MAXROW + 1], neg_max[:], q[:, :, at, MAXROW], ALU.subtract).then_inc(s["max_lo"], 1)

            def outputs(x, last_one):
                l, g, b, n = x
                if last_one is not None:
                    dve.wait_ge(s[f"attn{last_one.layer}"], GROUPS * last_one.seq + last_one.group + 1)
                dve.wait_ge(s["pv"], n + 1)
                dve.tensor_copy(o_sum[:], o_ps[:, :, :, HD + 1:VW]).then_inc(s["o_lo"], 1)
                dve.reciprocal(recip[:], o_ps[:, :, :, HD]).then_inc(s["recip"], 1)
                dve.wait_ge(s["o_lo"], n + 1)
                dve.tensor_tensor(o_sum[:], o_ps[:, :, :, 0:HD], o_sum[:], ALU.add).then_inc(s["o_sum"], 1)
                dve.wait_ge(s["o_sum"], n + 1)
                dve.wait_ge(s["recip"], n + 1)
                if g % 2 == 0 and (g or isinstance(b, int) and b):
                    dve.wait_ge(s[f"at_ps{l}"], 4 * b + g // 2)
                at = GROUP * HD * (g % 2)
                dst = attn[l][:, :, at:at + GROUP * HD].rearrange("p t (h d) -> p t h d", d=HD)
                dve.tensor_tensor(dst, o_sum[:], recip[:].unsqueeze(3).broadcast_to([P, TILES, GROUP, HD]), ALU.mult).then_inc(s[f"attn{l}"], 1)

            def chunk_lo(x):
                l, c = x.layer, x.group // 2
                dve.wait_ge(s[f"at_hi{l}"], 4 * x.seq + c + 1)
                dve.scalar_tensor_tensor(out=aT[l][:, 1, c, :], in0=psT[:, SEQ:2 * SEQ], scalar=XS, in1=aT[l][:, 0, c, :],
                                         op0=ALU.mult, op1=ALU.subtract).then_inc(s[f"at_lo{l}"], 1)

            def mix(b, e, t, ps):
                m = 16 * b + (2 * e + t)
                dve.wait_ge(s["expert"], m + 1)
                if e:
                    dve.wait_ge(s["mixed"], m - 1)
                dve.scalar_tensor_tensor(out=ffn[:, t, :], in0=ps, scalar=chosen[:, t, e:e + 1], in1=ffn[:, t, :],
                                         op0=ALU.mult, op1=ALU.add).then_inc(s["mixed"], 1)

            def constants():
                for i in range(2):
                    dve.memset(kT[i][64:P, :, 0, :], 0.0)
                    dve.memset(kT[i][0:64, :, 1, :], 0.0)
                for l in range(2):
                    dve.memset(vs[l][:, :, :, HD:HD + 1], 1.0)
                dve.memset(logits[1][:, :, LORA:8], NEG)
                dve.memset(ones[:], XS)
                dve.memset(w_b[64:P, 1, :], 0.0)

            constants()
            dve.wait_ge(s["x_rot"], 16)
            for t in range(TILES):
                norm_stats(0, 0, t)
            norm_var(0, 0)
            dve.wait_ge(s["ident"], 16)
            dve.tensor_copy(ident16[:], ident32[:])
            dve.tensor_copy(identb[:], ident32[:]).then_inc(s["made"], 1)
            for t in range(TILES):
                norm_x(0, 0, t)

            def run(before, these, after, jobs, first=False):
                turn, count = in_flight(before, these, after)
                jobs = placed(these, jobs)
                if not before:
                    k_turned(these[0])
                for k in range(count):
                    mine = jobs[k] if k < len(jobs) else [[], [], []]
                    if turn(k) is not None:
                        maxima(turn(k))
                        if turn(k + 1) is not None:
                            k_turned(turn(k + 1))
                        max_rows(turn(k))
                    for x in mine[0]:
                        job(*x)
                    if first and k < GROUPS:
                        split(split_by[2 * k + 1])
                    if turn(k - 2) is not None:
                        outputs(turn(k - 2), turn(k - 3) or (turns(0, 0, 0)[-1] if turn(k - 2).n == GROUPS else None))
                    if chunked(turn(k - 3)):
                        chunk_lo(turn(k - 3))
                    for x in mine[1]:
                        job(*x)
                    if first and k < GROUPS:
                        split(split_by[2 * k + 2])
                    for x in mine[2]:
                        job(*x)

            program(dve, job, run)

        @block.tensor
        def _(pe):
            pe.wait_ge(s["made"], 1)
            pe.wait_ge(s["masks"], 5)

            def product(out, lhs, t, w, lo, start=True, part=(0, PRODUCTS)):
                at = slice(t * P, (t + 1) * P)
                steps = [(c, i, j) for c in range(CH) for i, j in ((0, 0), (0, 1), (1, 0))]
                for c, i, j in steps[slice(*part)]:
                    last_ = pe.matmul(out, lhs[:, i, c, at], w[:, j, c, lo:lo + out.shape[1]], start=start and (c, i, j) == steps[0],
                                      stop=(c, i, j) == steps[-1])
                return last_

            def add_row(out, row):
                for j in range(2):
                    pe.matmul(out, ones[row:row + 1, :], bias[row:row + 1, j, 0:out.shape[1]], start=j == 0, stop=False)

            def turn_q(x):
                q, g = stacks(x.layer, x.seq)[0], x.group
                for j in range(PAIRS):
                    for t in range(TILES):
                        h = GROUP * g + 2 * j
                        last = pe.transpose(tT[:, j * SEQ + t * P:j * SEQ + (t + 1) * P],
                                            q[:, t, h:h + 2, :].rearrange("p h k -> p (h k)"), ident16[:])
                return last

            def turn_qk(x, first):
                l, g, b, n = x
                kk = stacks(l, b)[1]
                if g == 0:
                    pe.wait_ge(s[f"qk_lo{l}"], 4 * b + 4)
                    pe.wait_ge(s[f"cleared{l}"], 2 * b + 3)
                if not first or n:
                    pe.wait_ge(s["qm_t"], n if first else n - 1)
                turn_q(x)
                for t in range(TILES):
                    at = PAIRS * SEQ + t * P
                    if l == 0:
                        for j in range(PAIRS):
                            h = GROUP * g + 2 * j
                            last = pe.transpose(tT[:, at + j * SEQ:at + j * SEQ + P],
                                                kk[:, t, h:h + 2, :].rearrange("p h k -> p (h k)"), ident16[:])
                    else:
                        for r in range(2):
                            last = pe.transpose(tT[BLK * r:BLK * (r + 1), at:at + P], kk[:, t, g, :], ident16[:])
                last.then_inc(s["t1"], 1)

            def scores(x, between):
                l, k, _, n = x
                q, kk = qT[k % 2], kT[k % 2]
                pe.wait_ge(s["k_t"], n + 1)
                if positive(n):
                    pe.wait_ge(s["s_max"], 3 * n - 1)
                free(1 + k % 2)
                bank = psS[:, k % 2, :]
                pe.matmul(bank.rearrange("p (h k) -> p h k", h=GROUP), identb[:], mask_qk[:].unsqueeze(1).broadcast_to([P, GROUP, P]),
                          start=True, stop=False, skip_group_check=True)
                for j in range(PAIRS):
                    last = pe.matmul(bank[:, 2 * P * j:2 * P * (j + 1)].rearrange("p (h k) -> p h k", h=2), q[:, j, 0:P],
                                     kk[:, j if l == 0 else 0, :, 0:P], start=False, stop=True, skip_group_check=True)
                last.then_inc(s["s_ps"], 1)
                for j in range(PAIRS):
                    free(1 + (k + 1 + j) % 2)
                    if j:
                        between()
                    if j or positive(n):
                        pe.wait_ge(s["s_max"], 3 * n + j)
                    bank = psS[:, (k + 1 + j) % 2, :].rearrange("p (h k) -> p h k", h=2)
                    pe.matmul(bank[:, :, P:SEQ], identb[:], mask_qk[:].unsqueeze(1).broadcast_to([P, 2, P]), start=True, stop=False,
                              skip_group_check=True)
                    pe.matmul(bank, q[:, j, P:SEQ], kk[:, j if l == 0 else 0, :, :], start=False, stop=True,
                              skip_group_check=True).then_inc(s["s_ps"], 1)

            def scores_t(x):
                l, k, _, n = x
                kk = kT[k % 2]
                pe.wait_ge(s["qm_t"], n + 1)
                pe.wait_ge(s["p32"], n)
                for j in range(PAIRS):
                    out = psB[:, j, :].rearrange("p (h q) -> p h q", h=2)
                    pe.matmul(out[:, :, 0:P], identb[:], mask_kq[:].unsqueeze(1).broadcast_to([P, 2, P]), start=True, stop=False,
                              skip_group_check=True)
                    for h in range(2):
                        pe.matmul(out[:, h, :], kk[:, j if l == 0 else 0, h, 0:P], qmT[:, j, :], start=False, stop=True,
                                  skip_group_check=True)
                pe.matmul(psB[:, 2, :].rearrange("p (h q) -> p h q", h=GROUP), identb[:],
                          mask_kq[:].unsqueeze(1).broadcast_to([P, GROUP, P]), start=True, stop=False, skip_group_check=True)
                for j in range(PAIRS):
                    for h in range(2):
                        last = pe.matmul(psB[:, 2, P * (2 * j + h):P * (2 * j + h + 1)], kk[:, j if l == 0 else 0, h, P:SEQ],
                                         qmT[:, j, P:SEQ], start=False, stop=True, skip_group_check=True)
                last.then_inc(s["st"], 1)

            def values(x):
                l, g, b, n = x
                v_of = stacks(l, b)[2]
                pe.wait_ge(s["p_lo"], n + 1)
                if g == 0:
                    pe.wait_ge(s[f"v_lo{l}"], 2 * b + 2)
                if positive(n):
                    pe.wait_ge(s["o_sum"], n)
                for h in range(GROUP):
                    v = GROUP * g + h if l == 0 else g
                    for t in range(TILES):
                        for kt in range(t + 1):
                            at = SEQ * h + P * t if kt == 0 else GROUP * SEQ + P * h
                            pe.matmul(o_ps[:, t, h, :], p_hi[g % 2][:, at:at + P], v_of[:, kt, v, :], start=kt == 0, stop=False,
                                      skip_group_check=True)
                            last = pe.matmul(o_ps[:, t, h, 0:HD + 1], p_lo[:, at:at + P], v_of[:, kt, v, 0:HD + 1], start=False,
                                             stop=kt == t, skip_group_check=True)
                last.then_inc(s["pv"], 1)

            def turn_chunk(x):
                l, g, b, _ = x
                if g > 1:
                    pe.wait_ge(s[f"at_lo{l}"], 4 * b + g // 2)
                pe.wait_ge(s[f"attn{l}"], GROUPS * b + g + 1)
                for t in range(TILES):
                    last_ = pe.transpose(psT[:, SEQ + t * P:SEQ + (t + 1) * P], attn[l][:, t, :], ident32[:])
                last_.then_inc(s[f"at_ps{l}"], 1)

            def expert(ps, b, e, t, lo=0, hi=PRODUCTS):
                if lo == 0 and isinstance(b, int) and b == 0:
                    pe.wait_ge(s["w_lo"], until[f"exp{e}"])
                last_ = product(ps, xT[0], t, w_exp, 512 * e, part=(lo, hi))
                if hi == PRODUCTS:
                    last_.then_inc(s["expert"], 1)

            def taken(kind, *at):
                if kind == "turn":
                    l, b, t = at
                    return s[f"xt_lo{l}"], 2 * b + t + 1
                if kind == "small":
                    l, b = at
                    return (s["logits0"], 2 * b + 2) if l == 0 else (s["mid_raw"], 2 * b + 2)
                if kind == "proj":
                    l, b, t, part = at
                    return (s["v_lo0"], 2 * b + t + 1) if part == 2 else (s[f"rope{l}"], 4 * b + 2 * t + part + 1)
                if kind == "expert":
                    b, e, t = at
                    return s["mixed"], 16 * b + (2 * e + t + 1)
                if kind == "mid":
                    return s["midT"], at[0] + 1
                if kind == "chosen":
                    return s["chosenT"], at[0] + 1
                b, t = at
                return s[{"bias": "ffn_in", "out0": "weighed0", "delta": "gated1", "out1": "weighed1"}[kind]], 2 * b + t + 1

            def free(bank):
                if bank in held:
                    pe.wait_ge(*held.pop(bank))

            def large(x):
                return x[0] in ("expert", "proj", "out0", "out1")

            def job(bank, kind, *at, lo=0, hi=PRODUCTS):
                if not on_pe((kind, *at)):
                    return
                ps = bank_of[bank]
                half = ps.bitcast(F16)
                if lo == 0:
                    free(bank)
                if hi == PRODUCTS:
                    held[bank] = taken(kind, *at)
                if kind == "turn":
                    l, b, t = at
                    pe.wait_ge(s[f"xn{l}"], 2 * b + t + 1)
                    for c in range(CH):
                        last_ = pe.transpose(ps[:, c * P:(c + 1) * P], (rot_t, ffn)[l][:, t, c * P:(c + 1) * P], ident32[:])
                    last_.then_inc(s[f"xt_ps{l}"], 1)
                elif kind == "small":
                    l, b = at
                    if b0_first(l, b):
                        pe.wait_ge(s["w_lo"], until["small"])
                    pe.wait_ge(s[f"xt_lo{l}"], 2 * b + 2)
                    for t in range(TILES):
                        last_ = product(ps[:, slice(*small_at[l][t])], input_t(l, b), t, w_small, (0, ROUTER_AT)[l])
                    last_.then_inc(s[f"small{l}"], 1)
                elif kind == "proj":
                    l, b, t, part = at
                    w = 512 if l == 0 or part == 0 else 256
                    if lo == 0 and b0_first(0, b):
                        pe.wait_ge(s["w_lo"], until[f"qkv0_{part}"] if l == 0 else N)
                    if l == 1 and lo == 0:
                        add_row(ps[:, 0:w], (B_Q, B_KV)[part])
                    last_ = product(ps[:, 0:w], input_t(l, b), t, (w_qkv0, w_qkv1)[l], 512 * part, start=l == 0, part=(lo, hi))
                    if hi == PRODUCTS:
                        last_.then_inc(s["v_ps"] if l == 0 and part == 2 else s[f"proj{l}"], 1)
                elif kind == "chosen":
                    b, = at
                    pe.wait_ge(s["chosen"], b + 1)
                    for t in range(TILES):
                        last_ = pe.transpose(half[0:EXPERTS, t * P:(t + 1) * P], chosen16[:, t, :], ident16[:])
                    last_.then_inc(s["chosen_T"], 1)
                elif kind == "bias":
                    b, t = at
                    if b0_first(0, b):
                        pe.wait_ge(s["w_lo"], until["bias"])
                    pe.wait_ge(s["chosenT"], b + 1)
                    for j in range(2):
                        last_ = pe.matmul(ps, chosenT[:, t * P:(t + 1) * P], bias[0:EXPERTS, j, :], start=j == 0, stop=j == 1)
                    last_.then_inc(s["ffn_bias"], 1)
                elif kind == "expert":
                    expert(ps, *at, lo, hi)
                elif kind == "out0":
                    b, t = at
                    if lo == 0:
                        if b0_first(0, b):
                            pe.wait_ge(s["w_lo"], until["o0"])
                        pe.wait_ge(s["at_lo0"], 4 * b + 4)
                    last_ = product(ps, aT[0], t, w_o0, 0, part=(lo, hi))
                    if hi == PRODUCTS:
                        last_.then_inc(s["out0"], 1)
                elif kind == "mid":
                    b, = at
                    pe.wait_ge(s["mid_lo"], b + 1)
                    for t in range(TILES):
                        last_ = pe.transpose(half[:, t * P:(t + 1) * P], mid16[:, t, :, :].rearrange("p a n -> p (a n)"), ident16[:])
                    last_.then_inc(s["mid_ps"], 1)
                elif kind == "delta":
                    b, t = at
                    pe.wait_ge(s["midT"], b + 1)
                    for j in range(2):
                        last_ = pe.matmul(ps, midT[:, t * P:(t + 1) * P], w_b[:, j, :], start=j == 0, stop=j == 1)
                    last_.then_inc(s["delta"], 1)
                elif kind == "out1":
                    b, t = at
                    if lo == 0:
                        pe.wait_ge(s["at_lo1"], 4 * b + 4)
                        add_row(ps, B_O)
                    last_ = product(ps, aT[1], t, w_o1, 0, start=False, part=(lo, hi))
                    if hi == PRODUCTS:
                        last_.then_inc(s["out1"], 1)

            held = {}

            def b0_first(l, b):
                return l == 0 and isinstance(b, int) and b == 0

            def run(before, these, after, jobs, first=False):
                turn, count = in_flight(before, these, after)
                jobs = placed(these, jobs)
                if before:
                    held.clear()
                    for slot in placed(before[-GROUPS:], beside_first(before[0].seq)[-len(before):]):
                        for bank, *x in sum(slot, []):
                            if on_pe(x):
                                held[bank] = taken(*x)
                if not before:
                    if these[0].n:
                        pe.wait_ge(s["at_lo0"], 4)
                    turn_qk(these[0], True)
                for k in range(count):
                    mine = jobs[k] if k < len(jobs) else [[], [], []]
                    mine = [[x for x in y if on_pe(x[1:])] for y in mine]
                    cut = [x for x in mine[0][:1] if large(x[1:])] if turn(k) is not None else []
                    busy = bool(mine[1])

                    def between():
                        if turn(k + 1) is not None:
                            x = turn(k - 4)
                            if chunked(x):
                                pe.wait_ge(s[f"at_lo{x.layer}"], 4 * x.seq + x.group // 2 + 1)
                            turn_qk(turn(k + 1), False)
                        for x in cut:
                            job(*x, hi=FIRST)

                    if turn(k) is not None:
                        scores(turn(k), between)
                        for x in cut:
                            job(*x, lo=FIRST)
                        for x in mine[0][len(cut):]:
                            job(*x)
                    if turn(k - 2) is not None and (busy or turn(k) is None):
                        values(turn(k - 2))
                    if turn(k) is not None:
                        pe.wait_ge(s["max_lo"], turn(k).n + 1)
                        if turn(k + 1) is not None:
                            pe.wait_ge(s["k_t"], turn(k).n + 2)
                    if chunked(turn(k - 3)):
                        turn_chunk(turn(k - 3))
                    if turn(k) is not None:
                        turn_q(turn(k)).then_inc(s["t2"], 1)
                        if busy:
                            for x in mine[1]:
                                job(*x)
                        elif turn(k - 2) is not None:
                            values(turn(k - 2))
                        scores_t(turn(k))
                    for x in mine[2]:
                        job(*x)

            program(pe, job, run)


_OUT = (BATCH, SEQ, C)


def kernel(**inputs):
    import concourse.bacc as _bacc
    from concourse.bass_utils import run_bass_kernel_spmd as _run

    v = {k: np.asarray(w) for k, w in inputs.items()}
    rows = np.arange(W_QKV1).reshape(KV_HEADS, GROUP + 2, HD)
    order = np.concatenate([rows[:, :GROUP].ravel(), rows[:, GROUP].ravel(), rows[:, GROUP + 1].ravel()])
    t = np.arange(SEQ, dtype=np.float32)
    inv = (1.0 / 1000000.0 ** (np.arange(0, HD, 2, dtype=np.float32) / HD)).astype(np.float32)
    freq = np.outer(t, inv).astype(np.float32)

    def tiled(table):
        return np.ascontiguousarray(table.reshape(TILES, P, -1).transpose(1, 0, 2)).astype(np.float32)

    arrays = {
        "x": v["L0_attn_x"],
        "wqkv0": np.concatenate([v["L0_attn_wq"].T, v["L0_attn_wk"].T, v["L0_attn_wv"].T], axis=1),
        "wo0": v["L0_attn_wo"].T,
        "gate": v["L0_ffn_gate_w"].T,
        "gate_b": v["L0_ffn_gate_b"],
        "wexp": v["L0_ffn_expert_w"].reshape(-1, C).T,
        "expert_b": v["L0_ffn_expert_b"],
        "wqkv1": v["L1_attn_w_qkv"][order].T,
        "b_qkv1": v["L1_attn_b_qkv"][order][None, :],
        "wo1": v["L1_attn_w_dense"].T,
        "b_o1": v["L1_attn_b_dense"][None, :],
        "router": v["L1_ffn_router_w"].T,
        "A": v["L1_ffn_A"].reshape(-1, C).T,
        "B": v["L1_ffn_B"].transpose(0, 2, 1).reshape(-1, C),
        "ident": np.eye(P, dtype=np.float32),
        "rope0": tiled(np.stack([np.cos(t) * OUT, -np.sin(t) * OUT, np.sin(t) * OUT], axis=1)),
        "cos1": tiled(np.concatenate([np.cos(freq), np.cos(freq)], axis=1) * OUT),
        "sin1": tiled(np.concatenate([-np.sin(freq), np.sin(freq)], axis=1) * OUT),
        "iota8": np.tile(np.arange(8, dtype=np.float32), (P, 1)),
    }
    nc = _bacc.Bacc("TRN2", target_bir_lowering=False, num_devices=1)
    ins, aps = {}, {}
    for name, x in arrays.items():
        x = np.ascontiguousarray(x)
        ins["in_" + name] = x
        aps[name] = nc.dram_tensor("in_" + name, x.shape, mybir.dt.from_np(x.dtype), kind="ExternalInput").ap()
    aps["out"] = nc.dram_tensor("out", _OUT, F32, kind="ExternalOutput").ap()
    build(nc, aps)
    return _run(nc, [ins], core_ids=[0]).results[0]["out"]
```
